# Optimizing a Trainium2 kernel written in Bass

```python
import numpy as np
import jax
import jax.numpy as jnp

def _softmax(x, axis=-1):
    return jax.nn.softmax(x, axis=axis)
def _gelu(x):
    return jax.nn.gelu(x, approximate=True)
def _silu(x):
    return jax.nn.silu(x)
def _sigmoid(x):
    return jax.nn.sigmoid(x)
def _layernorm(x, axis=-1, eps=1e-5):
    m = jnp.mean(x, axis=axis, keepdims=True)
    v = jnp.var(x, axis=axis, keepdims=True)
    return (x - m) / jnp.sqrt(v + eps)
def _scatter_add(tgt, idx, src, axis=0):
    return tgt.at[idx].add(src)
def _segment_sum(src, seg, n):
    return jax.ops.segment_sum(src, seg, n)

kernel_name = 'mk_conv_preact_d4_conv_nhwc96_e064d3'

def setup_inputs(seed: int = 0):
    np.random.seed(seed)
    _w = jnp.asarray
    def _rec_inputs():
        import jax
        import jax.numpy as jnp
        _gk = jax.random.key(seed)
        x = -0.0005963 + 1.001 * jax.random.normal(jax.random.fold_in(_gk, 1), (8, 64, 64, 96), jnp.float32)
        return x
    x = _rec_inputs()
    def _L0_conv_setup():
        import jax, jax.numpy as jnp
        import numpy as np
        B, H, W, C = (8, 64, 64, 96)
        D_STATE = 16
        DT_RANK = 16
        D_INNER = int(C * 2.0)
        K = 4

        def _ss2d(x, in_proj_w, conv_w, conv_b, x_proj_w, dt_proj_w, dt_proj_b, A_logs, Ds, ln_gamma, ln_beta, out_proj_w):
            Bb, Hh, Ww, Cc = x.shape
            L = Hh * Ww
            xz = x @ in_proj_w.T
            xpart, z = jnp.split(xz, 2, axis=-1)
            xc = jnp.transpose(xpart, (0, 3, 1, 2))
            xc = jax.lax.conv_general_dilated(xc, conv_w, (1, 1), 'SAME', dimension_numbers=('NCHW', 'OIHW', 'NCHW'), feature_group_count=D_INNER)
            xc = jax.nn.silu(xc + conv_b[None, :, None, None])
            x_hw = xc.reshape(Bb, D_INNER, L)
            x_wh = jnp.transpose(xc, (0, 1, 3, 2)).reshape(Bb, D_INNER, L)
            xs = jnp.stack([x_hw, x_wh, x_hw[:, :, ::-1], x_wh[:, :, ::-1]], axis=1)
            x_dbl = jnp.einsum('bkdl,kcd->bkcl', xs, x_proj_w)
            dts, Bs, Cs = jnp.split(x_dbl, [DT_RANK, DT_RANK + D_STATE], axis=2)
            dts = jnp.einsum('bkrl,kdr->bkdl', dts, dt_proj_w)
            A = -jnp.exp(A_logs).reshape(K, D_INNER, D_STATE)
            delta = jax.nn.softplus(dts + dt_proj_b[None, :, :, None])
            u_l = jnp.transpose(xs, (3, 0, 1, 2))
            d_l = jnp.transpose(delta, (3, 0, 1, 2))
            B_l = jnp.transpose(Bs, (3, 0, 1, 2))
            C_l = jnp.transpose(Cs, (3, 0, 1, 2))

            def step(h, inp):
                u_t, d_t, b_t, c_t = inp
                dA = jnp.exp(d_t[..., None] * A[None])
                h = dA * h + (d_t * u_t)[..., None] * b_t[:, :, None, :]
                y = jnp.einsum('bkdn,bkn->bkd', h, c_t)
                return (h, y)
            h0 = jnp.zeros((Bb, K, D_INNER, D_STATE), x.dtype)
            _, ys = jax.lax.scan(step, h0, (u_l, d_l, B_l, C_l))
            ys = jnp.transpose(ys, (1, 2, 3, 0)) + Ds.reshape(K, D_INNER)[None, :, :, None] * xs
            y = ys[:, 0] + ys[:, 2, :, ::-1]
            y_wh = ys[:, 1] + ys[:, 3, :, ::-1]
            y = y + jnp.transpose(y_wh.reshape(Bb, D_INNER, Ww, Hh), (0, 1, 3, 2)).reshape(Bb, D_INNER, L)
            y = jnp.transpose(y.reshape(Bb, D_INNER, Hh, Ww), (0, 2, 3, 1))
            mu = y.mean(-1, keepdims=True)
            var = y.var(-1, keepdims=True)
            y = (y - mu) * jax.lax.rsqrt(var + 1e-05) * ln_gamma + ln_beta
            y = y * jax.nn.silu(z)
            return y @ out_proj_w.T
        key = jax.random.key(seed)
        ks = jax.random.split(key, 10)
        s = lambda k, shape, sc=0.02: jax.random.normal(k, shape, jnp.float32) * sc
        x = jax.random.normal(ks[0], (B, H, W, C), jnp.float32)
        in_proj_w = s(ks[1], (2 * D_INNER, C))
        conv_w = s(ks[2], (D_INNER, 1, 3, 3), 0.1)
        conv_b = jnp.zeros((D_INNER,), jnp.float32)
        x_proj_w = s(ks[3], (K, DT_RANK + 2 * D_STATE, D_INNER))
        dt_proj_w = s(ks[4], (K, D_INNER, DT_RANK), 0.1)
        dt_proj_b = jax.random.uniform(ks[5], (K, D_INNER), jnp.float32, -4.0, -2.0)
        A_logs = jnp.log(jnp.tile(jnp.arange(1.0, D_STATE + 1.0, dtype=jnp.float32), (K * D_INNER, 1)))
        Ds = jnp.ones((K * D_INNER,), jnp.float32)
        ln_gamma = jnp.ones((D_INNER,), jnp.float32)
        ln_beta = jnp.zeros((D_INNER,), jnp.float32)
        out_proj_w = s(ks[6], (C, D_INNER))
        return {'x': x, 'in_proj_w': in_proj_w, 'conv_w': conv_w, 'conv_b': conv_b, 'x_proj_w': x_proj_w, 'dt_proj_w': dt_proj_w, 'dt_proj_b': dt_proj_b, 'A_logs': A_logs, 'Ds': Ds, 'ln_gamma': ln_gamma, 'ln_beta': ln_beta, 'out_proj_w': out_proj_w}
    _L0_conv_all = _L0_conv_setup()
    _L0_conv_in = {k: v for k, v in _L0_conv_all.items() if k in ('in_proj_w', 'conv_w', 'conv_b', 'x_proj_w', 'dt_proj_w', 'dt_proj_b', 'A_logs', 'Ds', 'ln_gamma', 'ln_beta', 'out_proj_w', )}
    del _L0_conv_all

    def _L1_conv_setup():
        import jax, jax.numpy as jnp
        import numpy as np
        B, H, W = (2, 56, 56)
        D_MODEL, D_STATE, D_CONV, DT_RANK, K = (96, 16, 3, 6, 4)
        D_INNER = 192

        def _hscan1(x):
            cols = jnp.arange(x.shape[3]) % 2 == 1
            return jnp.where(cols[None, None, None, :], x[:, :, ::-1, :], x)

        def _vscan1(x):
            rows = jnp.arange(x.shape[2]) % 2 == 1
            x = jnp.where(rows[None, None, :, None], x[:, :, :, ::-1], x)
            return jnp.swapaxes(x, 2, 3)

        def _revert_vscan1(x):
            x = jnp.swapaxes(x, 2, 3)
            rows = jnp.arange(x.shape[2]) % 2 == 1
            return jnp.where(rows[None, None, :, None], x[:, :, :, ::-1], x)

        def _selective_scan(u, delta, A, Bs, Cs, D, delta_bias):
            Bb, KD, L = u.shape
            k = Bs.shape[1]
            d = KD // k
            N = A.shape[1]
            delta = jax.nn.softplus(delta + delta_bias[None, :, None])
            u4 = u.reshape(Bb, k, d, L)
            dt4 = delta.reshape(Bb, k, d, L)
            A4 = A.reshape(k, d, N)
            dA = jnp.exp(jnp.einsum('bkdl,kdn->lbkdn', dt4, A4))
            dBu = jnp.einsum('bkdl,bknl,bkdl->lbkdn', dt4, Bs, u4)
            Ct = jnp.transpose(Cs, (3, 0, 1, 2))
            h0 = jnp.zeros((Bb, k, d, N), u.dtype)

            def step(h, inp):
                dA_t, dBu_t, C_t = inp
                h = dA_t * h + dBu_t
                y = jnp.einsum('bkdn,bkn->bkd', h, C_t)
                return (h, y)
            _, ys = jax.lax.scan(step, h0, (dA, dBu, Ct))
            y = jnp.transpose(ys, (1, 2, 3, 0)).reshape(Bb, KD, L)
            return y + u * D[None, :, None]
        key = jax.random.key(seed)
        ks = jax.random.split(key, 8)
        s = 0.02
        return {'x': jax.random.normal(ks[0], (B, H, W, D_MODEL), jnp.float32), 'in_proj_w': jax.random.normal(ks[1], (2 * D_INNER, D_MODEL), jnp.float32) * s, 'conv_w': jax.random.normal(ks[2], (D_INNER, 1, D_CONV, D_CONV), jnp.float32) * s, 'conv_b': jnp.zeros((D_INNER,), jnp.float32), 'x_proj_weight': jax.random.normal(ks[3], (K, DT_RANK + 2 * D_STATE, D_INNER), jnp.float32) * s, 'dt_projs_weight': jax.random.normal(ks[4], (K, D_INNER, DT_RANK), jnp.float32) * DT_RANK ** (-0.5), 'dt_projs_bias': jax.random.uniform(ks[5], (K, D_INNER), jnp.float32, -4.6, -2.3), 'A_logs': jnp.log(jnp.tile(jnp.arange(1, D_STATE + 1, dtype=jnp.float32)[None, :], (K * D_INNER, 1))), 'Ds': jnp.ones((K * D_INNER,), jnp.float32), 'out_norm_w': jnp.ones((D_INNER,), jnp.float32), 'out_norm_b': jnp.zeros((D_INNER,), jnp.float32), 'out_proj_w': jax.random.normal(ks[6], (D_MODEL, D_INNER), jnp.float32) * s}
    _L1_conv_all = _L1_conv_setup()
    _L1_conv_in = {k: v for k, v in _L1_conv_all.items() if k in ('in_proj_w', 'conv_w', 'conv_b', 'x_proj_weight', 'dt_projs_weight', 'dt_projs_bias', 'A_logs', 'Ds', 'out_norm_w', 'out_norm_b', 'out_proj_w', )}
    del _L1_conv_all

    def _L2_conv_setup():
        import jax, jax.numpy as jnp
        import numpy as np
        B, H, W, C = (8, 64, 64, 96)
        D_STATE = 16
        D_INNER = 192
        DT_RANK = 6
        LN_EPS = 1e-05

        def _selective_scan(u, dt, A, Bm, Cm):
            uT = jnp.moveaxis(u, -1, 0)
            dtT = jnp.moveaxis(dt, -1, 0)
            BT = jnp.moveaxis(Bm, -1, 0)
            CT = jnp.moveaxis(Cm, -1, 0)

            def step(h, inp):
                u_l, dt_l, B_l, C_l = inp
                dA = jnp.exp(dt_l[..., None] * A[None])
                h = dA * h + (dt_l * u_l)[..., None] * B_l[:, :, None, :]
                y = jnp.einsum('bkdn,bkn->bkd', h, C_l)
                return (h, y)
            h0 = jnp.zeros(u.shape[:-1] + (A.shape[-1],), u.dtype)
            _, ys = jax.lax.scan(step, h0, (uT, dtT, BT, CT))
            return jnp.moveaxis(ys, 0, -1)

        def _forward_core(xc, x_proj_w, dt_projs_w, dt_projs_b, A_logs, Ds):
            b, c, h, w = xc.shape
            L = h * w
            x_hw = jnp.stack([xc.reshape(b, c, L), jnp.transpose(xc, (0, 1, 3, 2)).reshape(b, c, L)], axis=1)
            xs = jnp.concatenate([x_hw, jnp.flip(x_hw, axis=-1)], axis=1)
            x_dbl = jnp.einsum('bkdl,kcd->bkcl', xs, x_proj_w)
            dts = x_dbl[:, :, :DT_RANK]
            Bs = x_dbl[:, :, DT_RANK:DT_RANK + D_STATE]
            Cs = x_dbl[:, :, DT_RANK + D_STATE:]
            dts = jnp.einsum('bkrl,kdr->bkdl', dts, dt_projs_w)
            dt = jax.nn.softplus(dts + dt_projs_b[None, :, :, None])
            A = -jnp.exp(A_logs)
            out = _selective_scan(xs, dt, A, Bs, Cs) + Ds[None, :, :, None] * xs
            inv = jnp.flip(out[:, 2:4], axis=-1)
            wh = jnp.transpose(out[:, 1].reshape(b, c, w, h), (0, 1, 3, 2)).reshape(b, c, L)
            invwh = jnp.transpose(inv[:, 1].reshape(b, c, w, h), (0, 1, 3, 2)).reshape(b, c, L)
            return out[:, 0] + inv[:, 0] + wh + invwh
        key = jax.random.key(seed)
        ks = jax.random.split(key, 10)
        x = jax.random.normal(ks[0], (B, H, W, C), dtype=jnp.float32)
        in_proj_w = jax.random.normal(ks[1], (2 * D_INNER, C), dtype=jnp.float32) * 0.02
        conv_w = jax.random.normal(ks[2], (D_INNER, 1, 3, 3), dtype=jnp.float32) * 0.1
        conv_b = jax.random.normal(ks[3], (D_INNER,), dtype=jnp.float32) * 0.01
        x_proj_w = jax.random.normal(ks[4], (4, DT_RANK + 2 * D_STATE, D_INNER), dtype=jnp.float32) * 0.05
        dt_projs_w = jax.random.normal(ks[5], (4, D_INNER, DT_RANK), dtype=jnp.float32) * 0.1
        dt_projs_b = jax.random.normal(ks[6], (4, D_INNER), dtype=jnp.float32) * 0.01
        A_logs = jnp.log(jnp.tile(jnp.arange(1, D_STATE + 1, dtype=jnp.float32), (4, D_INNER, 1)))
        Ds = jnp.ones((4, D_INNER), dtype=jnp.float32)
        ln_g = jnp.ones((D_INNER,), dtype=jnp.float32)
        ln_b = jnp.zeros((D_INNER,), dtype=jnp.float32)
        out_proj_w = jax.random.normal(ks[7], (C, D_INNER), dtype=jnp.float32) * 0.02
        return dict(x=x, in_proj_w=in_proj_w, conv_w=conv_w, conv_b=conv_b, x_proj_w=x_proj_w, dt_projs_w=dt_projs_w, dt_projs_b=dt_projs_b, A_logs=A_logs, Ds=Ds, ln_g=ln_g, ln_b=ln_b, out_proj_w=out_proj_w)
    _L2_conv_all = _L2_conv_setup()
    _L2_conv_in = {k: v for k, v in _L2_conv_all.items() if k in ('in_proj_w', 'conv_w', 'conv_b', 'x_proj_w', 'dt_projs_w', 'dt_projs_b', 'A_logs', 'Ds', 'ln_g', 'ln_b', 'out_proj_w', )}
    del _L2_conv_all

    def _L3_conv_setup():
        import jax, jax.numpy as jnp
        import numpy as np

        def _mamba(u, W_in, conv_w, conv_b, W_x, W_dt, b_dt, A_log, D, W_out):
            Bsz, L, _ = u.shape
            d_inner, d_conv = conv_w.shape
            dt_rank = W_dt.shape[1]
            d_state = A_log.shape[1]
            xz = jnp.einsum('blc,ec->ble', u, W_in)
            xs, z = jnp.split(xz, 2, axis=-1)
            xp = jnp.pad(xs, ((0, 0), (d_conv - 1, 0), (0, 0)))
            xc = sum((xp[:, k:k + L, :] * conv_w[:, k] for k in range(d_conv))) + conv_b
            xc = jax.nn.silu(xc)
            dbc = jnp.einsum('bld,ed->ble', xc, W_x)
            dt = dbc[..., :dt_rank]
            Bm = dbc[..., dt_rank:dt_rank + d_state]
            Cm = dbc[..., dt_rank + d_state:]
            delta = jax.nn.softplus(jnp.einsum('blr,dr->bld', dt, W_dt) + b_dt)
            A = -jnp.exp(A_log)
            dA = jnp.exp(delta[..., None] * A)
            dBu = delta[..., None] * Bm[:, :, None, :] * xc[..., None]

            def step(h, inp):
                dA_t, dBu_t, C_t = inp
                h = dA_t * h + dBu_t
                y = jnp.einsum('bdn,bn->bd', h, C_t)
                return (h, y)
            h0 = jnp.zeros((Bsz, d_inner, d_state), u.dtype)
            _, ys = jax.lax.scan(step, h0, (jnp.swapaxes(dA, 0, 1), jnp.swapaxes(dBu, 0, 1), jnp.swapaxes(Cm, 0, 1)))
            y = jnp.swapaxes(ys, 0, 1) + xc * D
            y = y * jax.nn.silu(z)
            return jnp.einsum('bld,cd->blc', y, W_out)
        key = jax.random.key(seed)
        ks = jax.random.split(key, 8)
        B, H, W, d_model = (2, 96, 96, 96)
        d_state, d_conv, expand = (16, 3, 2)
        d_inner = expand * d_model
        dt_rank = -(-d_model // 16)
        x = jax.random.normal(ks[0], (B, H, W, d_model), jnp.float32)
        W_in = jax.random.normal(ks[1], (2 * d_inner, d_model), jnp.float32) * d_model ** (-0.5)
        conv_w = jax.random.normal(ks[2], (d_inner, d_conv), jnp.float32) * d_conv ** (-0.5)
        conv_b = jnp.zeros((d_inner,), jnp.float32)
        W_x = jax.random.normal(ks[3], (dt_rank + 2 * d_state, d_inner), jnp.float32) * d_inner ** (-0.5)
        W_dt = jax.random.normal(ks[4], (d_inner, dt_rank), jnp.float32) * dt_rank ** (-0.5)
        b_dt = jnp.log(jnp.expm1(jnp.full((d_inner,), 0.01, jnp.float32)))
        A_log = jnp.log(jnp.broadcast_to(jnp.arange(1, d_state + 1, dtype=jnp.float32), (d_inner, d_state)))
        D = jnp.ones((d_inner,), jnp.float32)
        W_out = jax.random.normal(ks[5], (d_model, d_inner), jnp.float32) * d_inner ** (-0.5)
        return {'x': x, 'W_in': W_in, 'conv_w': conv_w, 'conv_b': conv_b, 'W_x': W_x, 'W_dt': W_dt, 'b_dt': b_dt, 'A_log': A_log, 'D': D, 'W_out': W_out}
    _L3_conv_all = _L3_conv_setup()
    _L3_conv_in = {k: v for k, v in _L3_conv_all.items() if k in ('W_in', 'conv_w', 'conv_b', 'W_x', 'W_dt', 'b_dt', 'A_log', 'D', 'W_out', )}
    del _L3_conv_all

    return {
        "x": x,
        "L0_conv_in_proj_w": _L0_conv_in["in_proj_w"],
        "L0_conv_conv_w": _L0_conv_in["conv_w"],
        "L0_conv_conv_b": _L0_conv_in["conv_b"],
        "L0_conv_x_proj_w": _L0_conv_in["x_proj_w"],
        "L0_conv_dt_proj_w": _L0_conv_in["dt_proj_w"],
        "L0_conv_dt_proj_b": _L0_conv_in["dt_proj_b"],
        "L0_conv_A_logs": _L0_conv_in["A_logs"],
        "L0_conv_Ds": _L0_conv_in["Ds"],
        "L0_conv_ln_gamma": _L0_conv_in["ln_gamma"],
        "L0_conv_ln_beta": _L0_conv_in["ln_beta"],
        "L0_conv_out_proj_w": _L0_conv_in["out_proj_w"],
        "L1_conv_in_proj_w": _L1_conv_in["in_proj_w"],
        "L1_conv_conv_w": _L1_conv_in["conv_w"],
        "L1_conv_conv_b": _L1_conv_in["conv_b"],
        "L1_conv_x_proj_weight": _L1_conv_in["x_proj_weight"],
        "L1_conv_dt_projs_weight": _L1_conv_in["dt_projs_weight"],
        "L1_conv_dt_projs_bias": _L1_conv_in["dt_projs_bias"],
        "L1_conv_A_logs": _L1_conv_in["A_logs"],
        "L1_conv_Ds": _L1_conv_in["Ds"],
        "L1_conv_out_norm_w": _L1_conv_in["out_norm_w"],
        "L1_conv_out_norm_b": _L1_conv_in["out_norm_b"],
        "L1_conv_out_proj_w": _L1_conv_in["out_proj_w"],
        "L2_conv_in_proj_w": _L2_conv_in["in_proj_w"],
        "L2_conv_conv_w": _L2_conv_in["conv_w"],
        "L2_conv_conv_b": _L2_conv_in["conv_b"],
        "L2_conv_x_proj_w": _L2_conv_in["x_proj_w"],
        "L2_conv_dt_projs_w": _L2_conv_in["dt_projs_w"],
        "L2_conv_dt_projs_b": _L2_conv_in["dt_projs_b"],
        "L2_conv_A_logs": _L2_conv_in["A_logs"],
        "L2_conv_Ds": _L2_conv_in["Ds"],
        "L2_conv_ln_g": _L2_conv_in["ln_g"],
        "L2_conv_ln_b": _L2_conv_in["ln_b"],
        "L2_conv_out_proj_w": _L2_conv_in["out_proj_w"],
        "L3_conv_W_in": _L3_conv_in["W_in"],
        "L3_conv_conv_w": _L3_conv_in["conv_w"],
        "L3_conv_conv_b": _L3_conv_in["conv_b"],
        "L3_conv_W_x": _L3_conv_in["W_x"],
        "L3_conv_W_dt": _L3_conv_in["W_dt"],
        "L3_conv_b_dt": _L3_conv_in["b_dt"],
        "L3_conv_A_log": _L3_conv_in["A_log"],
        "L3_conv_D": _L3_conv_in["D"],
        "L3_conv_W_out": _L3_conv_in["W_out"],
    }

def reference(x, L0_conv_in_proj_w, L0_conv_conv_w, L0_conv_conv_b, L0_conv_x_proj_w, L0_conv_dt_proj_w, L0_conv_dt_proj_b, L0_conv_A_logs, L0_conv_Ds, L0_conv_ln_gamma, L0_conv_ln_beta, L0_conv_out_proj_w, L1_conv_in_proj_w, L1_conv_conv_w, L1_conv_conv_b, L1_conv_x_proj_weight, L1_conv_dt_projs_weight, L1_conv_dt_projs_bias, L1_conv_A_logs, L1_conv_Ds, L1_conv_out_norm_w, L1_conv_out_norm_b, L1_conv_out_proj_w, L2_conv_in_proj_w, L2_conv_conv_w, L2_conv_conv_b, L2_conv_x_proj_w, L2_conv_dt_projs_w, L2_conv_dt_projs_b, L2_conv_A_logs, L2_conv_Ds, L2_conv_ln_g, L2_conv_ln_b, L2_conv_out_proj_w, L3_conv_W_in, L3_conv_conv_w, L3_conv_conv_b, L3_conv_W_x, L3_conv_W_dt, L3_conv_b_dt, L3_conv_A_log, L3_conv_D, L3_conv_W_out):
    import jax
    import jax.numpy as jnp
    def _L0_conv_ref(x, in_proj_w, conv_w, conv_b, x_proj_w, dt_proj_w, dt_proj_b, A_logs, Ds, ln_gamma, ln_beta, out_proj_w):
        import jax, jax.numpy as jnp
        import numpy as np
        B, H, W, C = (8, 64, 64, 96)
        D_STATE = 16
        DT_RANK = 16
        D_INNER = int(C * 2.0)
        K = 4

        def _ss2d(x, in_proj_w, conv_w, conv_b, x_proj_w, dt_proj_w, dt_proj_b, A_logs, Ds, ln_gamma, ln_beta, out_proj_w):
            Bb, Hh, Ww, Cc = x.shape
            L = Hh * Ww
            xz = x @ in_proj_w.T
            xpart, z = jnp.split(xz, 2, axis=-1)
            xc = jnp.transpose(xpart, (0, 3, 1, 2))
            xc = jax.lax.conv_general_dilated(xc, conv_w, (1, 1), 'SAME', dimension_numbers=('NCHW', 'OIHW', 'NCHW'), feature_group_count=D_INNER)
            xc = jax.nn.silu(xc + conv_b[None, :, None, None])
            x_hw = xc.reshape(Bb, D_INNER, L)
            x_wh = jnp.transpose(xc, (0, 1, 3, 2)).reshape(Bb, D_INNER, L)
            xs = jnp.stack([x_hw, x_wh, x_hw[:, :, ::-1], x_wh[:, :, ::-1]], axis=1)
            x_dbl = jnp.einsum('bkdl,kcd->bkcl', xs, x_proj_w)
            dts, Bs, Cs = jnp.split(x_dbl, [DT_RANK, DT_RANK + D_STATE], axis=2)
            dts = jnp.einsum('bkrl,kdr->bkdl', dts, dt_proj_w)
            A = -jnp.exp(A_logs).reshape(K, D_INNER, D_STATE)
            delta = jax.nn.softplus(dts + dt_proj_b[None, :, :, None])
            u_l = jnp.transpose(xs, (3, 0, 1, 2))
            d_l = jnp.transpose(delta, (3, 0, 1, 2))
            B_l = jnp.transpose(Bs, (3, 0, 1, 2))
            C_l = jnp.transpose(Cs, (3, 0, 1, 2))

            def step(h, inp):
                u_t, d_t, b_t, c_t = inp
                dA = jnp.exp(d_t[..., None] * A[None])
                h = dA * h + (d_t * u_t)[..., None] * b_t[:, :, None, :]
                y = jnp.einsum('bkdn,bkn->bkd', h, c_t)
                return (h, y)
            h0 = jnp.zeros((Bb, K, D_INNER, D_STATE), x.dtype)
            _, ys = jax.lax.scan(step, h0, (u_l, d_l, B_l, C_l))
            ys = jnp.transpose(ys, (1, 2, 3, 0)) + Ds.reshape(K, D_INNER)[None, :, :, None] * xs
            y = ys[:, 0] + ys[:, 2, :, ::-1]
            y_wh = ys[:, 1] + ys[:, 3, :, ::-1]
            y = y + jnp.transpose(y_wh.reshape(Bb, D_INNER, Ww, Hh), (0, 1, 3, 2)).reshape(Bb, D_INNER, L)
            y = jnp.transpose(y.reshape(Bb, D_INNER, Hh, Ww), (0, 2, 3, 1))
            mu = y.mean(-1, keepdims=True)
            var = y.var(-1, keepdims=True)
            y = (y - mu) * jax.lax.rsqrt(var + 1e-05) * ln_gamma + ln_beta
            y = y * jax.nn.silu(z)
            return y @ out_proj_w.T
        return _ss2d(x, in_proj_w, conv_w, conv_b, x_proj_w, dt_proj_w, dt_proj_b, A_logs, Ds, ln_gamma, ln_beta, out_proj_w)

    def _L1_conv_ref(x, in_proj_w, conv_w, conv_b, x_proj_weight, dt_projs_weight, dt_projs_bias, A_logs, Ds, out_norm_w, out_norm_b, out_proj_w):
        import jax, jax.numpy as jnp
        import numpy as np
        B, H, W = (2, 56, 56)
        D_MODEL, D_STATE, D_CONV, DT_RANK, K = (96, 16, 3, 6, 4)
        D_INNER = 192

        def _hscan1(x):
            cols = jnp.arange(x.shape[3]) % 2 == 1
            return jnp.where(cols[None, None, None, :], x[:, :, ::-1, :], x)

        def _vscan1(x):
            rows = jnp.arange(x.shape[2]) % 2 == 1
            x = jnp.where(rows[None, None, :, None], x[:, :, :, ::-1], x)
            return jnp.swapaxes(x, 2, 3)

        def _revert_vscan1(x):
            x = jnp.swapaxes(x, 2, 3)
            rows = jnp.arange(x.shape[2]) % 2 == 1
            return jnp.where(rows[None, None, :, None], x[:, :, :, ::-1], x)

        def _selective_scan(u, delta, A, Bs, Cs, D, delta_bias):
            Bb, KD, L = u.shape
            k = Bs.shape[1]
            d = KD // k
            N = A.shape[1]
            delta = jax.nn.softplus(delta + delta_bias[None, :, None])
            u4 = u.reshape(Bb, k, d, L)
            dt4 = delta.reshape(Bb, k, d, L)
            A4 = A.reshape(k, d, N)
            dA = jnp.exp(jnp.einsum('bkdl,kdn->lbkdn', dt4, A4))
            dBu = jnp.einsum('bkdl,bknl,bkdl->lbkdn', dt4, Bs, u4)
            Ct = jnp.transpose(Cs, (3, 0, 1, 2))
            h0 = jnp.zeros((Bb, k, d, N), u.dtype)

            def step(h, inp):
                dA_t, dBu_t, C_t = inp
                h = dA_t * h + dBu_t
                y = jnp.einsum('bkdn,bkn->bkd', h, C_t)
                return (h, y)
            _, ys = jax.lax.scan(step, h0, (dA, dBu, Ct))
            y = jnp.transpose(ys, (1, 2, 3, 0)).reshape(Bb, KD, L)
            return y + u * D[None, :, None]
        Bb, Hh, Ww, _ = x.shape
        L = Hh * Ww
        xz = jnp.einsum('bhwc,ec->bhwe', x, in_proj_w)
        xc, z = jnp.split(xz, 2, axis=-1)
        xc = jnp.transpose(xc, (0, 3, 1, 2))
        xc = jax.lax.conv_general_dilated(xc, conv_w, (1, 1), ((1, 1), (1, 1)), feature_group_count=D_INNER)
        xc = jax.nn.silu(xc + conv_b[None, :, None, None])
        x1 = _hscan1(xc)
        x_hw = x1.reshape(Bb, 1, D_INNER, L)
        x2 = _vscan1(x1)
        x_wh = x2.reshape(Bb, 1, D_INNER, L)
        xs = jnp.concatenate([x_hw, x_wh, x_hw[..., ::-1], x_wh[..., ::-1]], axis=1)
        x_dbl = jnp.einsum('bkdl,kcd->bkcl', xs, x_proj_weight)
        dts, Bs, Cs = jnp.split(x_dbl, [DT_RANK, DT_RANK + D_STATE], axis=2)
        dts = jnp.einsum('bkrl,kdr->bkdl', dts, dt_projs_weight)
        u = xs.reshape(Bb, K * D_INNER, L)
        delta = dts.reshape(Bb, K * D_INNER, L)
        A = -jnp.exp(A_logs)
        out_y = _selective_scan(u, delta, A, Bs, Cs, Ds, dt_projs_bias.reshape(-1))
        oy = out_y.reshape(Bb, K, D_INNER, L)
        s0 = _hscan1(oy[:, 0].reshape(Bb, D_INNER, Hh, Ww))
        s2 = _hscan1(oy[:, 2, :, ::-1].reshape(Bb, D_INNER, Hh, Ww))
        s1 = _hscan1(_revert_vscan1(oy[:, 1].reshape(Bb, D_INNER, Ww, Hh)))
        s3 = _hscan1(_revert_vscan1(oy[:, 3, :, ::-1].reshape(Bb, D_INNER, Ww, Hh)))
        y = (s0 + s1 + s2 + s3).reshape(Bb, D_INNER, L)
        y = jnp.transpose(y, (0, 2, 1))
        mu = jnp.mean(y, axis=-1, keepdims=True)
        var = jnp.var(y, axis=-1, keepdims=True)
        y = (y - mu) / jnp.sqrt(var + 1e-05) * out_norm_w + out_norm_b
        y = y.reshape(Bb, Hh, Ww, D_INNER) * jax.nn.silu(z)
        return jnp.einsum('bhwd,cd->bhwc', y, out_proj_w)

    def _L2_conv_ref(x, in_proj_w, conv_w, conv_b, x_proj_w, dt_projs_w, dt_projs_b, A_logs, Ds, ln_g, ln_b, out_proj_w):
        import jax, jax.numpy as jnp
        import numpy as np
        B, H, W, C = (8, 64, 64, 96)
        D_STATE = 16
        D_INNER = 192
        DT_RANK = 6
        LN_EPS = 1e-05

        def _selective_scan(u, dt, A, Bm, Cm):
            uT = jnp.moveaxis(u, -1, 0)
            dtT = jnp.moveaxis(dt, -1, 0)
            BT = jnp.moveaxis(Bm, -1, 0)
            CT = jnp.moveaxis(Cm, -1, 0)

            def step(h, inp):
                u_l, dt_l, B_l, C_l = inp
                dA = jnp.exp(dt_l[..., None] * A[None])
                h = dA * h + (dt_l * u_l)[..., None] * B_l[:, :, None, :]
                y = jnp.einsum('bkdn,bkn->bkd', h, C_l)
                return (h, y)
            h0 = jnp.zeros(u.shape[:-1] + (A.shape[-1],), u.dtype)
            _, ys = jax.lax.scan(step, h0, (uT, dtT, BT, CT))
            return jnp.moveaxis(ys, 0, -1)

        def _forward_core(xc, x_proj_w, dt_projs_w, dt_projs_b, A_logs, Ds):
            b, c, h, w = xc.shape
            L = h * w
            x_hw = jnp.stack([xc.reshape(b, c, L), jnp.transpose(xc, (0, 1, 3, 2)).reshape(b, c, L)], axis=1)
            xs = jnp.concatenate([x_hw, jnp.flip(x_hw, axis=-1)], axis=1)
            x_dbl = jnp.einsum('bkdl,kcd->bkcl', xs, x_proj_w)
            dts = x_dbl[:, :, :DT_RANK]
            Bs = x_dbl[:, :, DT_RANK:DT_RANK + D_STATE]
            Cs = x_dbl[:, :, DT_RANK + D_STATE:]
            dts = jnp.einsum('bkrl,kdr->bkdl', dts, dt_projs_w)
            dt = jax.nn.softplus(dts + dt_projs_b[None, :, :, None])
            A = -jnp.exp(A_logs)
            out = _selective_scan(xs, dt, A, Bs, Cs) + Ds[None, :, :, None] * xs
            inv = jnp.flip(out[:, 2:4], axis=-1)
            wh = jnp.transpose(out[:, 1].reshape(b, c, w, h), (0, 1, 3, 2)).reshape(b, c, L)
            invwh = jnp.transpose(inv[:, 1].reshape(b, c, w, h), (0, 1, 3, 2)).reshape(b, c, L)
            return out[:, 0] + inv[:, 0] + wh + invwh
        b, h, w, _ = x.shape
        xz = x @ in_proj_w.T
        xp, z = jnp.split(xz, 2, axis=-1)
        xc = jnp.transpose(xp, (0, 3, 1, 2))
        xc = jax.lax.conv_general_dilated(xc, conv_w, (1, 1), ((1, 1), (1, 1)), feature_group_count=D_INNER, dimension_numbers=('NCHW', 'OIHW', 'NCHW'))
        xc = jax.nn.silu(xc + conv_b[None, :, None, None])
        y = _forward_core(xc, x_proj_w, dt_projs_w, dt_projs_b, A_logs, Ds)
        y = jnp.transpose(y, (0, 2, 1)).reshape(b, h, w, D_INNER)
        mu = jnp.mean(y, axis=-1, keepdims=True)
        var = jnp.mean((y - mu) ** 2, axis=-1, keepdims=True)
        y = (y - mu) * jax.lax.rsqrt(var + LN_EPS) * ln_g + ln_b
        y = y * jax.nn.silu(z)
        return y @ out_proj_w.T

    def _L3_conv_ref(x, W_in, conv_w, conv_b, W_x, W_dt, b_dt, A_log, D, W_out):
        import jax, jax.numpy as jnp
        import numpy as np

        def _mamba(u, W_in, conv_w, conv_b, W_x, W_dt, b_dt, A_log, D, W_out):
            Bsz, L, _ = u.shape
            d_inner, d_conv = conv_w.shape
            dt_rank = W_dt.shape[1]
            d_state = A_log.shape[1]
            xz = jnp.einsum('blc,ec->ble', u, W_in)
            xs, z = jnp.split(xz, 2, axis=-1)
            xp = jnp.pad(xs, ((0, 0), (d_conv - 1, 0), (0, 0)))
            xc = sum((xp[:, k:k + L, :] * conv_w[:, k] for k in range(d_conv))) + conv_b
            xc = jax.nn.silu(xc)
            dbc = jnp.einsum('bld,ed->ble', xc, W_x)
            dt = dbc[..., :dt_rank]
            Bm = dbc[..., dt_rank:dt_rank + d_state]
            Cm = dbc[..., dt_rank + d_state:]
            delta = jax.nn.softplus(jnp.einsum('blr,dr->bld', dt, W_dt) + b_dt)
            A = -jnp.exp(A_log)
            dA = jnp.exp(delta[..., None] * A)
            dBu = delta[..., None] * Bm[:, :, None, :] * xc[..., None]

            def step(h, inp):
                dA_t, dBu_t, C_t = inp
                h = dA_t * h + dBu_t
                y = jnp.einsum('bdn,bn->bd', h, C_t)
                return (h, y)
            h0 = jnp.zeros((Bsz, d_inner, d_state), u.dtype)
            _, ys = jax.lax.scan(step, h0, (jnp.swapaxes(dA, 0, 1), jnp.swapaxes(dBu, 0, 1), jnp.swapaxes(Cm, 0, 1)))
            y = jnp.swapaxes(ys, 0, 1) + xc * D
            y = y * jax.nn.silu(z)
            return jnp.einsum('bld,cd->blc', y, W_out)
        B, H, W, C = x.shape
        y = _mamba(x.reshape(B, H * W, C), W_in, conv_w, conv_b, W_x, W_dt, b_dt, A_log, D, W_out)
        return y.reshape(B, H, W, C)

    def _gn(v, G=32, eps=1e-5):
        B_, H_, W_, C_ = v.shape
        g = v.reshape(B_, H_, W_, G, C_ // G)
        m = jnp.mean(g, axis=(1, 2, 4), keepdims=True)
        s = jnp.var(g, axis=(1, 2, 4), keepdims=True)
        return ((g - m) / jnp.sqrt(s + eps)).reshape(v.shape)

    def _ln_c(v, eps=1e-6):
        m = jnp.mean(v, axis=-1, keepdims=True)
        s = jnp.var(v, axis=-1, keepdims=True)
        return (v - m) / jnp.sqrt(s + eps)

    def _ln_t(v, eps=1e-5):
        m = jnp.mean(v, axis=-1, keepdims=True)
        s = jnp.var(v, axis=-1, keepdims=True)
        return (v - m) / jnp.sqrt(s + eps)

    def _to_tokens(v):
        B_, H_, W_, C_ = v.shape
        return v.reshape(B_, H_ * W_, C_)
    def _from_tokens(t, like):
        return t.reshape(like.shape)

    x = x + _L0_conv_ref(_gn(x), L0_conv_in_proj_w, L0_conv_conv_w, L0_conv_conv_b, L0_conv_x_proj_w, L0_conv_dt_proj_w, L0_conv_dt_proj_b, L0_conv_A_logs, L0_conv_Ds, L0_conv_ln_gamma, L0_conv_ln_beta, L0_conv_out_proj_w)
    x = x + _L1_conv_ref(_gn(x), L1_conv_in_proj_w, L1_conv_conv_w, L1_conv_conv_b, L1_conv_x_proj_weight, L1_conv_dt_projs_weight, L1_conv_dt_projs_bias, L1_conv_A_logs, L1_conv_Ds, L1_conv_out_norm_w, L1_conv_out_norm_b, L1_conv_out_proj_w)
    x = x + _L2_conv_ref(_gn(x), L2_conv_in_proj_w, L2_conv_conv_w, L2_conv_conv_b, L2_conv_x_proj_w, L2_conv_dt_projs_w, L2_conv_dt_projs_b, L2_conv_A_logs, L2_conv_Ds, L2_conv_ln_g, L2_conv_ln_b, L2_conv_out_proj_w)
    x = x + _L3_conv_ref(_gn(x), L3_conv_W_in, L3_conv_conv_w, L3_conv_conv_b, L3_conv_W_x, L3_conv_W_dt, L3_conv_b_dt, L3_conv_A_log, L3_conv_D, L3_conv_W_out)
    return x


_drawn_inputs = setup_inputs


def setup_inputs(seed=0):
    import zlib

    import numpy as np

    out = dict(_drawn_inputs(seed))
    spreads = {'L0_conv_conv_b': (0.0, 0.1),
     'L0_conv_Ds': (1.0, 0.6),
     'L0_conv_ln_gamma': (1.0, 0.6),
     'L0_conv_ln_beta': (0.0, 0.8),
     'L1_conv_conv_b': (0.0, 0.1),
     'L1_conv_Ds': (1.0, 0.6),
     'L1_conv_out_norm_w': (1.0, 0.6),
     'L1_conv_out_norm_b': (0.0, 0.8),
     'L2_conv_Ds': (1.0, 0.6),
     'L2_conv_ln_g': (1.0, 0.6),
     'L2_conv_ln_b': (0.0, 0.8),
     'L3_conv_conv_b': (0.0, 0.1),
     'L3_conv_b_dt': (-4.600166320800781, 0.6),
     'L3_conv_D': (1.0, 0.2)}
    factors = {'L0_conv_conv_w': 3.726,
     'L0_conv_x_proj_w': 8.0,
     'L0_conv_dt_proj_w': 8.0,
     'L0_conv_dt_proj_b': 8.0,
     'L0_conv_A_logs': 8.0,
     'L1_conv_conv_w': 8.0,
     'L1_conv_x_proj_weight': 8.0,
     'L1_conv_dt_projs_weight': 8.0,
     'L1_conv_dt_projs_bias': 8.0,
     'L1_conv_A_logs': 8.0,
     'L2_conv_conv_b': 8.0,
     'L2_conv_x_proj_w': 8.0,
     'L2_conv_dt_projs_w': 8.0,
     'L2_conv_dt_projs_b': 8.0,
     'L2_conv_A_logs': 8.0}
    for name, (base, spread) in spreads.items():
        noise = np.random.default_rng([zlib.crc32(name.encode()), seed]).standard_normal(out[name].shape)
        drawn = base * np.exp(spread * noise) if base else spread * noise
        out[name] = jnp.asarray(drawn.astype(out[name].dtype))
    for name, factor in factors.items():
        out[name] = (out[name] * factor).astype(out[name].dtype)
    return out
```

```python
from contextlib import ExitStack

import numpy as np

import concourse.bass as bass
from concourse import mybir

F32 = mybir.dt.float32
BF16 = mybir.dt.bfloat16
ALU = mybir.AluOpType
ACT = mybir.ActivationFunctionType

P = 128
NBATCH, SIDE, DM = 8, 64, 96
L = SIDE * SIDE
DI = 2 * DM
NS = 16
RMAX = 16
PAIRS = NBATCH // 2
TILES = 3
BANK = 512
BANKS_L = L // BANK
ROWS_PER_BANK = BANK // SIDE
CH = 1024
HALVES = CH // BANK
NCH = L // CH
PAD = SIDE + 2
GN_EPS = LN_EPS = 1e-5

KINDS = ["cross", "snake", "cross", "causal"]
DIRS = {"cross": 4, "snake": 4, "causal": 1}

STEPS = TILES * NS
LAST_USE = (2, 1, 3)
LAG, C_LAG = 4, 3
XDBL_AFTER, DELTA_AFTER = 2, 6
STORE_AT = 1


def first_order(kind, natural, rows=(0, SIDE)):
    a, b = rows
    if kind != "snake":
        return [(slice(0, SIDE), natural[:, a:b, :])]
    lo, hi = SIDE - 1 - a, SIDE - 1 - b
    flipped = natural[:, lo:(hi if hi >= 0 else None):-1, 1::2]
    return [(slice(0, None, 2), natural[:, a:b, 0::2]), (slice(1, None, 2), flipped)]


def column_order(kind, image):
    if kind != "snake":
        return [(slice(0, SIDE), image.rearrange("p h w -> p w h"))]
    return [(slice(0, None, 2), image[:, 0::2, :].rearrange("p h w -> p w h")),
            (slice(1, None, 2), image[:, 1::2, ::-1].rearrange("p h w -> p w h"))]


def stage_semaphores(nc, ctx, names):
    return {n: ctx.enter_context(nc.semaphore(n)) for n in names.split()}


def clear(nc, sem):
    for s in sem.values():
        nc.sync.sem_clear(s)
    nc.all_engine_barrier()


def to_channels_stage(nc, T, x_in, x_t):
    names = ("tokens_in transposed copied tokens_used stored")
    blocks = L // P
    with ExitStack() as ctx:
        sem = stage_semaphores(nc, ctx, names)
        tokens = ctx.enter_context(nc.sbuf_tensor("tokens", [P, blocks, DM], F32))
        chan = ctx.enter_context(nc.sbuf_tensor("chan", [DM, L], F32))
        ps = ctx.enter_context(nc.psum_tensor("ps_t", [P, 2, BANK], F32))
        with nc.Block() as block:
            @block.sync
            def _(sp):
                with sp.Fori(0, NBATCH) as b:
                    sp.wait_ge(sem["tokens_used"], b + 1)
                    sp.dma_start(tokens[:], x_in[b].rearrange("(q n) c -> q n c", q=P)).then_inc(sem["tokens_in"], 16)
                    sp.wait_ge(sem["copied"], b * BANKS_L + BANKS_L + 2)
                    sp.dma_start(x_t[b], chan[:]).then_inc(sem["stored"], 16)
                sp.wait_ge(sem["stored"], 16 * (NBATCH + 1))

            @block.tensor
            def _(pe):
                pe.sem_inc(sem["tokens_used"], 1)
                with pe.Fori(0, NBATCH) as b:
                    pe.wait_ge(sem["tokens_in"], b * 16 + 16)
                    for c in range(BANKS_L):
                        pe.wait_ge(sem["copied"], b * BANKS_L + (c + 1))
                        for j in range(4):
                            mm = pe.transpose(ps[0:DM, c % 2, j * P:(j + 1) * P], tokens[:, 4 * c + j, :],
                                              T["ident"][:, :])
                            if j == 3:
                                mm.then_inc(sem["transposed"], 1)
                    pe.wait_ge(sem["transposed"], b * BANKS_L + BANKS_L)
                    pe.sem_inc(sem["tokens_used"], 1)

            @block.scalar
            def _(act):
                act.sem_inc(sem["copied"], 2)
                act.sem_inc(sem["stored"], 16)
                with act.Fori(0, NBATCH) as b:
                    act.wait_ge(sem["stored"], b * 16 + 16)
                    for c in range(BANKS_L):
                        act.wait_ge(sem["transposed"], b * BANKS_L + (c + 1))
                        act.copy(chan[:].rearrange("d (q n) -> d n q", n=blocks)[:, 4 * c:4 * c + 4, :],
                                 ps[0:DM, c % 2, :].rearrange("d (n q) -> d n q", q=P)).then_inc(sem["copied"], 1)
        clear(nc, sem)


def setup_stage(nc, T, W, layers, neg_a):
    names = ("logs_in exp_done neg_done stored")
    with ExitStack() as ctx:
        sem = stage_semaphores(nc, ctx, names)
        cols = [DIRS[KINDS[n]] * TILES * NS for n in layers]
        logs = [ctx.enter_context(nc.sbuf_tensor(f"logs{n}", [P, c], F32)) for n, c in zip(layers, cols)]
        with nc.Block() as block:
            @block.sync
            def _(sp):
                for n, t in zip(layers, logs):
                    sp.dma_start(t[:], W[n]["a_log"]).then_inc(sem["logs_in"], 16)
                for i, (n, t) in enumerate(zip(layers, logs)):
                    sp.wait_ge(sem["neg_done"], i + 1)
                    sp.dma_start(neg_a[n].rearrange("k p c -> p k c"),
                                 t[:].rearrange("p (k c) -> p k c", c=TILES * NS)).then_inc(sem["stored"], 16)
                sp.wait_ge(sem["stored"], 16 * len(layers))

            @block.scalar
            def _(act):
                act.wait_ge(sem["logs_in"], 16 * len(layers))
                for t in logs:
                    act.activation(t[:], t[:], ACT.Exp).then_inc(sem["exp_done"], 1)

            @block.vector
            def _(dve):
                for i, t in enumerate(logs):
                    dve.wait_ge(sem["exp_done"], i + 1)
                    dve.tensor_scalar(t[:], t[:], -1.0, None, ALU.mult).then_inc(sem["neg_done"], 1)
        clear(nc, sem)


def expand_stage(nc, kind, T, W, x_t, useq, zgate):
    K = DIRS[kind]
    causal = kind == "causal"
    TAPS = 3 if causal else 9
    xp_shape = [P, L + 2] if causal else [P, PAD * PAD]
    DCH = 2 * BANKS_L + 2 + 5
    CONVS = TILES * TAPS
    names = ("w_in x_in stats stats_seen free_seen aggr group_ps centred sqrt_done scale_ready normed ps_full ps_free padded "
             "pad_full conv_step conv_free silu_done rotated z_full x_free seq_out small z_out")
    with ExitStack() as ctx:
        sem = stage_semaphores(nc, ctx, names)
        def sb(name, shape, dt=F32):
            return ctx.enter_context(nc.sbuf_tensor(name + W["tag"], shape, dt))
        win = sb("win", [DM, 2 * DI])
        convw = sb("convw", [P, TILES * TAPS])
        convb = sb("convb", [P, TILES])
        xn = sb("xn", [DM, 2, L])
        bn = sb("bn", [DM, 2, BANKS_L, 6])
        mv = sb("mv", [DM, 2, 2])
        gmean, dev, var, rstd, nbias = (sb(n, [DM, 2]) for n in ("gmean", "dev", "gvar", "grstd", "gnbias"))
        xp = [sb(f"xp{j}", xp_shape) for j in range(2)]
        acc = [sb(f"acc{j}", [P, L]) for j in range(2)]
        zb = sb("zb", [P, L])
        us = [sb(f"us{k}", [P, L]) for k in range(K)]
        ps = ctx.enter_context(nc.psum_tensor("ps_e" + W["tag"], [P, 4, BANK], F32))
        psg = ctx.enter_context(nc.psum_tensor("ps_g" + W["tag"], [P, BANK], F32))

        useq_v = useq.rearrange("(k p c) t q l -> k p c t q l", p=PAIRS, c=NCH)
        PER = TILES * 2 * BANKS_L

        def interior(t, c):
            if causal:
                return xp[t % 2][:, 2 + c * BANK:2 + (c + 1) * BANK]
            img = xp[t % 2][:].rearrange("p (h w) -> p h w", h=PAD)
            return img[:, 1 + c * ROWS_PER_BANK:1 + (c + 1) * ROWS_PER_BANK, 1:1 + SIDE]

        with nc.Block() as block:
            @block.sync
            def _(sp):
                sp.dma_start(win[:], W["win"]).then_inc(sem["w_in"], 16)
                sp.dma_start(convw[:], W["convw"]).then_inc(sem["w_in"], 16)
                sp.dma_start(convb[:], W["convb"]).then_inc(sem["w_in"], 16)

                def load_x(p):
                    sp.dma_start(xn[:], x_t[bass.ds(2 * p, 2)].rearrange("b c l -> c b l")).then_inc(sem["x_in"], 16)

                load_x(0)
                with sp.Fori(0, PAIRS) as p:
                    for t in range(TILES):
                        sp.wait_ge(sem["z_full"], p * TILES + (t + 1))
                        sp.dma_start(zgate[p, :, t].rearrange("c q l -> q c l"),
                                     zb[:].rearrange("q (c l) -> q c l", l=BANK)).then_inc(sem["z_out"], 16)
                        if t == TILES - 1:
                            sp.wait_ge(sem["x_free"], p + 1)
                            load_x((p + 1) % PAIRS)
                        sp.wait_ge(sem["silu_done"], p * TILES + (t + 3))
                        for k in range(K):
                            if k:
                                sp.wait_ge(sem["rotated"], p * (TILES * (K - 1)) + (t * (K - 1) + k))
                            sp.dma_start(useq_v[k, p, :, t].rearrange("c q l -> q c l"),
                                         us[k][:].rearrange("q (c l) -> q c l", l=CH)).then_inc(sem["seq_out"], 16)
                sp.wait_ge(sem["x_in"], 16 * (PAIRS + 1))
                sp.wait_ge(sem["z_out"], 16 * (PAIRS * TILES + 1))
                sp.wait_ge(sem["seq_out"], 16 * K * (PAIRS * TILES + 1))

            @block.tensor
            def _(pe):
                pe.wait_ge(sem["w_in"], 48)
                with pe.Fori(0, PAIRS) as p:
                    pe.wait_ge(sem["aggr"], p + 1)
                    pe.matmul(psg[0:DM, 0:2], T["group"][:, :], mv[:, :, 0], start=True, stop=True)\
                        .then_inc(sem["group_ps"], 1)
                    pe.wait_ge(sem["centred"], p + 1)
                    pe.matmul(psg[0:DM, 2:4], T["group"][:, :], var[:, :], start=True, stop=True)\
                        .then_inc(sem["group_ps"], 1)
                    pe.wait_ge(sem["normed"], p * 2 + 2)
                    m = 0
                    for t in range(TILES):
                        for which in range(2):
                            for c in range(BANKS_L):
                                cols = slice(c * BANK, (c + 1) * BANK)
                                pe.wait_ge(sem["ps_free"], p * PER + (m + 1))
                                o = which * DI
                                if t != 1:
                                    mm = pe.matmul(ps[:, m % 4, :], win[:, o:o + P], xn[:, t // 2, cols],
                                                   start=True, stop=True)
                                else:
                                    for b in range(2):
                                        mm = pe.matmul(ps[64 * b:64 * b + 64, m % 4, :], win[:, o + P:o + DI],
                                                       xn[:, b, cols], start=True, stop=True)
                                mm.then_inc(sem["ps_full"], 1)
                                m += 1
                    pe.wait_ge(sem["ps_full"], p * PER + PER)
                    pe.sem_inc(sem["x_free"], 1)

            @block.scalar
            def _(act):
                act.sem_inc(sem["ps_free"], 4)
                act.sem_inc(sem["silu_done"], 2)
                act.sem_inc(sem["z_out"], 16)
                act.sem_inc(sem["seq_out"], 16 * K)
                act.wait_ge(sem["w_in"], 48)
                act.wait_ge(sem["padded"], 2)
                with act.Fori(0, PAIRS) as p:
                    act.wait_ge(sem["small"], p * 5 + 4)
                    act.activation(rstd[:], rstd[:], ACT.Sqrt).then_inc(sem["sqrt_done"], 1)
                    act.wait_ge(sem["scale_ready"], p + 1)
                    for b in range(2):
                        act.activation(xn[:, b, :], xn[:, b, :], ACT.Identity, bias=nbias[:, b:b + 1],
                                       scale=rstd[:, b:b + 1]).then_inc(sem["normed"], 1)
                    m = 0

                    def take(t, which):
                        nonlocal m
                        for c in range(BANKS_L):
                            act.wait_ge(sem["ps_full"], p * PER + (m + 1))
                            if which == 0:
                                if c == 0:
                                    act.wait_ge(sem["conv_free"], p * TILES + LAST_USE[t])
                                src = ps[:, m % 4, :]
                                if not causal:
                                    src = src.rearrange("p (h w) -> p h w", w=SIDE)
                                ins = act.copy(interior(t, c), src)
                                ins.then_inc(sem["ps_free"], 1)
                            else:
                                if c == 0:
                                    act.wait_ge(sem["z_out"], p * (16 * TILES) + 16 * (t + 1))
                                img = ps[:, m % 4, :].rearrange("p (h w) -> p h w", w=SIDE)
                                dst = zb[:].rearrange("p (h w) -> p h w", w=SIDE)
                                a = c * ROWS_PER_BANK
                                if kind != "snake":
                                    parts = [(dst[:, a:a + ROWS_PER_BANK, :], img)]
                                else:
                                    lo = SIDE - 1 - a
                                    hi = lo - ROWS_PER_BANK
                                    parts = [(dst[:, a:a + ROWS_PER_BANK, 0::2], img[:, :, 0::2]),
                                             (dst[:, lo:(hi if hi >= 0 else None):-1, 1::2], img[:, :, 1::2])]
                                for d, s in parts:
                                    ins = act.activation(d, s, ACT.Silu)
                                ins.then_inc(sem["ps_free"], 1)
                            m += 1
                        act.wait_ge(sem["ps_free"], p * PER + (m + 4))
                        act.sem_inc(sem["pad_full"] if which == 0 else sem["z_full"], 1)

                    def first_sequence(t):
                        act.wait_ge(sem["conv_step"], p * CONVS + (t + 1) * TAPS)
                        act.wait_ge(sem["seq_out"], p * (16 * K * TILES) + 16 * K * (t + 1))
                        src = acc[t % 2][:].rearrange("p (h w) -> p h w", w=SIDE)
                        dst = us[0][:].rearrange("p (h w) -> p h w", w=SIDE)
                        parts = first_order(kind, src)
                        for j, (cols, view) in enumerate(parts):
                            ins = act.activation(dst[:, :, cols], view, ACT.Silu, bias=convb[:, t:t + 1])
                        ins.then_inc(sem["silu_done"], 1)

                    take(0, 0)
                    take(0, 1)
                    take(1, 0)
                    take(1, 1)
                    first_sequence(0)
                    take(2, 0)
                    take(2, 1)
                    first_sequence(1)
                    first_sequence(2)

            @block.vector
            def _(dve):
                for j in range(2):
                    dve.memset(xp[j][:], 0.0).then_inc(sem["padded"], 1)
                dve.sem_inc(sem["conv_free"], 2)
                dve.wait_ge(sem["padded"], 2)
                dve.wait_ge(sem["w_in"], 48)
                with dve.Fori(0, PAIRS) as p:
                    dve.wait_ge(sem["x_in"], p * 16 + 16)
                    for b in range(2):
                        for c in range(BANKS_L):
                            dve.bn_stats(bn[:, b, c, :], xn[:, b, c * BANK:(c + 1) * BANK]).then_inc(sem["stats"], 1)
                    dve.wait_ge(sem["stats"], p * (2 * BANKS_L) + 2 * BANKS_L)
                    dve.sem_inc(sem["stats_seen"], 1)
                    dve.bn_aggr(mv[:, 0, :], bn[:, 0].rearrange("p c s -> p (c s)"))
                    dve.bn_aggr(mv[:, 1, :], bn[:, 1].rearrange("p c s -> p (c s)")).then_inc(sem["aggr"], 1)
                    dve.wait_ge(sem["group_ps"], p * 2 + 1)
                    dve.tensor_copy(gmean[:], psg[0:DM, 0:2]).then_inc(sem["small"], 1)
                    dve.wait_ge(sem["small"], p * 5 + 1)
                    dve.tensor_tensor(dev[:], mv[:, :, 0], gmean[:], ALU.subtract).then_inc(sem["small"], 1)
                    dve.wait_ge(sem["small"], p * 5 + 2)
                    dve.tensor_tensor(dev[:], dev[:], dev[:], ALU.mult).then_inc(sem["small"], 1)
                    dve.wait_ge(sem["small"], p * 5 + 3)
                    dve.tensor_tensor(var[:], dev[:], mv[:, :, 1], ALU.add).then_inc(sem["centred"], 1)
                    dve.wait_ge(sem["group_ps"], p * 2 + 2)
                    dve.tensor_scalar(rstd[:], psg[0:DM, 2:4], GN_EPS, None, ALU.add).then_inc(sem["small"], 1)
                    dve.wait_ge(sem["sqrt_done"], p + 1)
                    dve.reciprocal(rstd[:], rstd[:]).then_inc(sem["small"], 1)
                    dve.wait_ge(sem["small"], p * 5 + 5)
                    dve.scalar_tensor_tensor(out=nbias[:], in0=gmean[:], scalar=-1.0, in1=rstd[:], op0=ALU.mult,
                                             op1=ALU.mult).then_inc(sem["scale_ready"], 1)
                    for t in range(TILES):
                        dve.wait_ge(sem["pad_full"], p * TILES + (t + 1))
                        dve.wait_ge(sem["silu_done"], p * TILES + LAST_USE[t])
                        a = acc[t % 2][:] if causal else acc[t % 2][:].rearrange("p (h w) -> p h w", w=SIDE)
                        for tap in range(TAPS):
                            if causal:
                                src = xp[t % 2][:, tap:tap + L]
                            else:
                                dy, dx = tap // 3, tap % 3
                                src = xp[t % 2][:].rearrange("p (h w) -> p h w", h=PAD)[:, dy:dy + SIDE, dx:dx + SIDE]
                            w = convw[:, t * TAPS + tap:t * TAPS + tap + 1]
                            if tap == 0:
                                dve.tensor_scalar(a, src, w, None, ALU.mult).then_inc(sem["conv_step"], 1)
                            else:
                                dve.wait_ge(sem["conv_step"], p * CONVS + (t * TAPS + tap))
                                dve.scalar_tensor_tensor(out=a, in0=src, scalar=w, in1=a, op0=ALU.mult,
                                                         op1=ALU.add).then_inc(sem["conv_step"], 1)
                        dve.wait_ge(sem["conv_step"], p * CONVS + (t + 1) * TAPS)
                        dve.sem_inc(sem["conv_free"], 1)

            @block.gpsimd
            def _(pool):
                if K == 1:
                    return
                with pool.Fori(0, PAIRS) as p:
                    for t in range(TILES):
                        pool.wait_ge(sem["silu_done"], p * TILES + (t + 3))
                        r = p * (TILES * (K - 1)) + t * (K - 1)
                        pool.wait_ge(sem["seq_out"], p * (16 * K * TILES) + 16 * K * (t + 1))
                        pool.sem_inc(sem["free_seen"], 1)
                        img = us[0][:].rearrange("p (h w) -> p h w", w=SIDE)
                        col = us[1][:].rearrange("p (w h) -> p w h", h=SIDE)
                        for rows, view in column_order(kind, img):
                            ins = pool.tensor_copy(col[:, :, rows], view)
                        ins.then_inc(sem["rotated"], 1)
                        pool.tensor_copy(us[2][:], us[0][:, ::-1]).then_inc(sem["rotated"], 1)
                        pool.wait_ge(sem["rotated"], r + 1)
                        pool.sem_inc(sem["free_seen"], 1)
                        pool.tensor_copy(us[3][:], us[1][:, ::-1]).then_inc(sem["rotated"], 1)
        clear(nc, sem)


def scan_stage(nc, kind, T, W, useq, neg_a, yseq):
    K = DIRS[kind]
    G = K * PAIRS
    NC = G * NCH
    BODY_CHUNKS = 2
    BS = BODY_CHUNKS * STEPS
    BT = BODY_CHUNKS * TILES

    events = []
    for q in range(BODY_CHUNKS):
        for t in range(TILES):
            for n in range(NS):
                events.append(("step", q, t, n))
                if t == TILES - 1 and n == XDBL_AFTER:
                    events.append(("xdbl", q + 1, 0, 0))
                if n == DELTA_AFTER:
                    events.append(("delta", q + (t + 1) // TILES, (t + 1) % TILES, 0))
    NE = len(events)

    def step_of(e):
        return e[1] * STEPS + e[2] * NS + e[3]

    names = ("pick_in x_full b_full c_full b_multiplied c_copied decay_ready h_ready state_saved "
             "state_zeroed gated reduced delta_full raw_ready clamped exp_ready log_ready softplus_step "
             "delta_ready du_ready split_hi dts_ready rest_ready split_mid split_lo stacked y_copied "
             "y_even y_odd zeroed")
    with ExitStack() as ctx:
        sem = stage_semaphores(nc, ctx, names)
        def sb(name, shape, dt=F32):
            return ctx.enter_context(nc.sbuf_tensor(name + W["tag"], shape, dt))
        pick = sb("pick", [96, TILES, NS, P], BF16)
        u = [sb(f"u{j}", [P, TILES, CH]) for j in range(2)]
        wx = [sb(f"wx{j}", [P, TILES, 96]) for j in range(2)]
        wdt = [sb(f"wdt{j}", [32, TILES, P]) for j in range(2)]
        bdt = [sb(f"bdt{j}", [P, TILES]) for j in range(2)]
        na = [sb(f"na{j}", [P, TILES * NS]) for j in range(2)]
        bc = [sb(f"bc{j}", [96, 2, CH], BF16) for j in range(2)]
        hi, mid, lo = (sb(n, [64, CH], BF16) for n in ("hi", "mid", "lo"))
        rest = sb("rest", [64, CH])
        dts = [sb(f"dts{j}", [32, CH]) for j in range(2)]
        raw, clamp, ex, ln, one = (sb(n, [P, CH]) for n in ("raw", "clamp", "ex", "ln", "one"))
        delta = [sb(f"delta{j}", [P, CH]) for j in range(2)]
        du = [sb(f"du{j}", [P, CH]) for j in range(2)]
        decay = [sb(f"decay{j}", [P, CH]) for j in range(2)]
        dbu = [sb(f"dbu{j}", [P, CH]) for j in range(2)]
        h = [sb(f"h{j}", [P, CH]) for j in range(3)]
        csb = [sb(f"csb{j}", [P, CH]) for j in range(2)]
        gh = [sb(f"gh{j}", [P, CH]) for j in range(2)]
        state = sb("state", [P, TILES * NS])
        nothing = sb("nothing", [P, 1])
        ybuf = [sb(f"ybuf{j}", [P, CH]) for j in range(2)]
        slot = [ctx.enter_context(nc.psum_tensor(f"slot{j}" + W["tag"], [P, CH], F32)) for j in range(2)]
        psc = ctx.enter_context(nc.psum_tensor("psc" + W["tag"], [P, CH], F32))
        psy = ctx.enter_context(nc.psum_tensor("psy" + W["tag"], [P, CH], F32))

        def halves():
            return [slice(a * BANK, (a + 1) * BANK) for a in range(HALVES)]


        with nc.Block() as block:
            @block.sync
            def _(sp):
                def load(C, j):
                    sp.dma_start(u[j][:], useq[C].rearrange("t q l -> q t l")).then_inc(sem["x_full"], 16)
                    k = C // (PAIRS * NCH)
                    sp.dma_start(wx[j][:], W["wx"][k]).then_inc(sem["x_full"], 16)
                    sp.dma_start(wdt[j][:], W["wdt"][k]).then_inc(sem["x_full"], 16)
                    sp.dma_start(bdt[j][:], W["bdt"][k]).then_inc(sem["x_full"], 16)
                    sp.dma_start(na[j][:], neg_a[k]).then_inc(sem["x_full"], 16)

                def stack(C, j):
                    for n, (part, ready) in enumerate([(hi, sem["split_hi"]), (mid, sem["split_mid"]), (lo, sem["split_lo"])]):
                        sp.wait_ge(ready, C + 1)
                        for s in range(2):
                            sp.dma_start(bc[j][32 * n:32 * n + 32, s, :], part[32 * s:32 * s + 32, :])\
                                .then_inc(sem["stacked"], 16)

                load(0, 0)
                sp.dma_start(pick[:], W["pick"].bitcast(BF16)).then_inc(sem["pick_in"], 16)
                stack(0, 0)
                with sp.Fori(0, NC // BODY_CHUNKS) as i:
                    for q in range(BODY_CHUNKS):
                        C = i * BODY_CHUNKS + q
                        sp.wait_ge(sem["h_ready"], C * STEPS + 2)
                        load((C + 1) % NC, (q + 1) % 2)
                        for t in range(TILES):
                            if t == TILES - 1:
                                stack(C + 1, (q + 1) % 2)
                            sp.wait_ge(sem["y_copied"], C * TILES + (t + 2))
                            j = (q * TILES + t) % 2
                            sp.dma_start(yseq[C, t], ybuf[j][:]).then_inc(sem["y_even"] if j == 0 else sem["y_odd"], 16)
                sp.wait_ge(sem["y_even"], 8 * NC * TILES + 16)
                sp.wait_ge(sem["y_odd"], 8 * NC * TILES + 32)
                sp.wait_ge(sem["x_full"], 80 * (NC + 1))
                sp.wait_ge(sem["stacked"], 96 * (NC + 1))

            @block.tensor
            def _(pe):
                def x_dbl(C, j, slot_j):
                    pe.wait_ge(sem["x_full"], C * 80 + 80)
                    for cols in halves():
                        for t in range(TILES):
                            mm = pe.matmul(slot[slot_j][0:96, cols], wx[j][:, t, :], u[j][:, t, cols],
                                           start=(t == 0), stop=(t == TILES - 1))
                    mm.then_inc(sem["b_full"], 1)

                def wait_released(e, C0):
                    kind_, q, t, n = e
                    if kind_ == "step":
                        pe.wait_ge(sem["b_multiplied"], C0 * STEPS + (step_of(e) + 1))
                    elif kind_ == "delta":
                        pe.wait_ge(sem["raw_ready"], C0 * TILES + (q * TILES + t + 1))
                    else:
                        pe.wait_ge(sem["dts_ready"], C0 + (q + 1))
                        pe.wait_ge(sem["rest_ready"], C0 + (q + 1))

                def issue(e, C0, v):
                    kind_, q, t, n = e
                    if kind_ == "xdbl":
                        x_dbl(C0 + q, q % 2, v % 2)
                    elif kind_ == "delta":
                        pe.wait_ge(sem["dts_ready"], C0 + (q + 1))
                        for cols in halves():
                            mm = pe.matmul(slot[v % 2][:, cols], wdt[q % 2][:, t, :], dts[q % 2][:, cols],
                                           start=True, stop=True)
                        mm.then_inc(sem["b_full"], 1)
                    else:
                        if t == 0 and n == 0:
                            pe.wait_ge(sem["stacked"], C0 * 96 + 96 * (q + 1))
                        for cols in halves():
                            mm = pe.matmul(slot[v % 2][:, cols], pick[:, t, n, :], bc[q % 2][:, 0, cols],
                                           start=True, stop=True)
                        mm.then_inc(sem["b_full"], 1)

                def broadcast_c(e, C0):
                    kind_, q, t, n = e
                    if kind_ != "step":
                        return
                    pe.wait_ge(sem["c_copied"], C0 * STEPS + (step_of(e) + 1))
                    for cols in halves():
                        mm = pe.matmul(psc[:, cols], pick[:, t, n, :], bc[q % 2][:, 1, cols],
                                       start=True, stop=True)
                    mm.then_inc(sem["c_full"], 1)

                def reduce(e, C0):
                    kind_, q, t, n = e
                    if kind_ != "step":
                        return
                    S = C0 * STEPS + step_of(e)
                    pe.wait_ge(sem["gated"], S + 4)
                    if n == 0:
                        pe.wait_ge(sem["y_copied"], C0 * TILES + (q * TILES + t + 1))
                    for cols in halves():
                        mm = pe.matmul(psy[:, cols], T["ident"][:, :], gh[step_of(e) % 2][:, cols],
                                       start=(n == 0), stop=(n == NS - 1), skip_group_check=True)
                    mm.then_inc(sem["reduced"], 1)

                pe.wait_ge(sem["zeroed"], 1)
                for cols in halves():
                    mm = pe.matmul(psy[:, cols], T["ident"][:, :], gh[0][:, cols], start=True, stop=True)
                mm.then_inc(sem["reduced"], 2)
                issue(("xdbl", 0, 0, 0), 0, 0)
                issue(("delta", 0, 0, 0), 0, 1)
                pe.wait_ge(sem["pick_in"], 16)
                for v in range(LAG):
                    if v < 2:
                        wait_released([("xdbl", 0, 0, 0), ("delta", 0, 0, 0)][v], 0)
                    else:
                        wait_released(events[v - 2], 0)
                    issue(events[v], 0, v)
                    if v < C_LAG:
                        broadcast_c(events[v], 0)
                with pe.Fori(0, G * NCH // BODY_CHUNKS) as i:
                    C0 = i * BODY_CHUNKS
                    for v in range(NE):
                        reduce(events[v], C0)
                        w = v + C_LAG
                        broadcast_c(events[w % NE], C0 + BODY_CHUNKS * (w // NE))
                        w = v + LAG
                        prev = events[(w - 2) % NE]
                        wait_released(prev, C0 + BODY_CHUNKS * ((w - 2) // NE))
                        issue(events[w % NE], C0 + BODY_CHUNKS * (w // NE), w)

            @block.vector
            def _(dve):
                def multiply(e, C0, v):
                    _, q, t, n = e
                    s = step_of(e)
                    S = C0 * STEPS + s
                    T_ = q * TILES + t
                    dve.wait_ge(sem["b_full"], C0 * (NE // BODY_CHUNKS) + (v + 3))
                    if n == 0:
                        dve.wait_ge(sem["du_ready"], C0 * TILES + (T_ + 1))
                    dve.wait_ge(sem["h_ready"], S + 1)
                    dve.tensor_tensor(dbu[s % 2][:], du[T_ % 2][:], slot[v % 2][:], ALU.mult)\
                        .then_inc(sem["b_multiplied"], 1)

                def scan(e, C0, g):
                    _, q, t, n = e
                    s = step_of(e)
                    S = C0 * STEPS + s
                    dve.wait_ge(sem["decay_ready"], S + 1)
                    dve.wait_ge(sem["b_multiplied"], S + 1)
                    dve.wait_ge(sem["gated"], S + 1)
                    dve.wait_ge(sem["state_saved"], S + 1)
                    if q == 0 and t == 0 and n == 0:
                        dve.wait_ge(sem["state_zeroed"], g + 1)
                    k = t * NS + n
                    dve.tensor_tensor_scan(h[s % 3][:], decay[s % 2][:], dbu[s % 2][:], state[:, k:k + 1],
                                           ALU.mult, ALU.add).then_inc(sem["h_ready"], 1)

                def remainder(C, v):
                    dve.wait_ge(sem["split_hi"], C + 1)
                    dve.tensor_tensor(rest[:], slot[v % 2][0:64, :], hi[:], ALU.subtract).then_inc(sem["rest_ready"], 1)

                def last_part(C):
                    dve.wait_ge(sem["split_mid"], C + 1)
                    dve.tensor_tensor(lo[:], rest[:], mid[:], ALU.subtract).then_inc(sem["split_lo"], 1)

                def clamp_raw(TT):
                    dve.wait_ge(sem["raw_ready"], TT + 1)
                    dve.tensor_scalar(clamp[:], raw[:], 30.0, None, ALU.min).then_inc(sem["clamped"], 1)

                def softplus(TT, T_):
                    dve.wait_ge(sem["exp_ready"], TT + 1)
                    dve.tensor_scalar(one[:], ex[:], 1.0, 1.0, ALU.min, ALU.add).then_inc(sem["softplus_step"], 1)
                    dve.wait_ge(sem["softplus_step"], TT * 3 + 1)
                    dve.scalar_tensor_tensor(out=one[:], in0=one[:], scalar=1.0, in1=ex[:], op0=ALU.subtract,
                                             op1=ALU.subtract).then_inc(sem["softplus_step"], 1)
                    dve.wait_ge(sem["softplus_step"], TT * 3 + 2)
                    dve.wait_ge(sem["log_ready"], TT + 1)
                    dve.scalar_tensor_tensor(out=one[:], in0=one[:], scalar=-1.2e-7, in1=ln[:], op0=ALU.max,
                                             op1=ALU.subtract).then_inc(sem["softplus_step"], 1)
                    dve.wait_ge(sem["softplus_step"], TT * 3 + 3)
                    dve.scalar_tensor_tensor(out=delta[T_ % 2][:], in0=one[:], scalar=-1.0, in1=raw[:],
                                             op0=ALU.mult, op1=ALU.max).then_inc(sem["delta_ready"], 1)

                dve.sem_inc(sem["h_ready"], 2)
                dve.memset(gh[0][:], 0.0).then_inc(sem["zeroed"], 1)
                remainder(0, 0)
                last_part(0)
                clamp_raw(0)
                softplus(0, 0)
                multiply(events[0], 0, 0)
                per_g = NCH // BODY_CHUNKS
                with dve.Fori(0, G) as g:
                    with dve.Fori(0, per_g) as half:
                        C0 = (g * per_g + half) * BODY_CHUNKS
                        for v, e in enumerate(events):
                            if e[0] == "xdbl":
                                remainder(C0 + e[1], v)
                                continue
                            if e[0] == "delta":
                                clamp_raw(C0 * TILES + (e[1] * TILES + e[2]))
                                continue
                            _, q, t, n = e
                            w = v + 1
                            while events[w % NE][0] != "step":
                                w += 1
                            multiply(events[w % NE], C0 + BODY_CHUNKS * (w // NE), w % NE)
                            scan(e, C0, g)
                            if t == TILES - 1 and n == XDBL_AFTER + 2:
                                last_part(C0 + (q + 1))
                            if n == DELTA_AFTER + 3:
                                T_ = q * TILES + t + 1
                                softplus(C0 * TILES + T_, T_)
                dve.wait_ge(sem["b_full"], NC // BODY_CHUNKS * NE + 2 + LAG - 1)
                dve.sem_inc(sem["b_multiplied"], 1)

            @block.scalar
            def _(act):
                def decay_of(e, C0):
                    _, q, t, n = e
                    s = step_of(e)
                    if n == 0:
                        act.wait_ge(sem["delta_ready"], C0 * TILES + (q * TILES + t + 1))
                    act.wait_ge(sem["h_ready"], C0 * STEPS + (s + 1))
                    k = t * NS + n
                    act.activation(decay[s % 2][:], delta[(q * TILES + t) % 2][:], ACT.Exp,
                                   scale=na[q % 2][:, k:k + 1]).then_inc(sem["decay_ready"], 1)

                def copy_c(e, C0):
                    s = step_of(e)
                    S = C0 * STEPS + s
                    act.wait_ge(sem["c_full"], S + 1)
                    act.wait_ge(sem["gated"], S + 2)
                    act.copy(csb[s % 2][:], psc[:]).then_inc(sem["c_copied"], 1)

                def save(e, C0):
                    s = step_of(e)
                    k = e[2] * NS + e[3]
                    act.wait_ge(sem["h_ready"], C0 * STEPS + (s + 3))
                    act.copy(state[:, k:k + 1], h[s % 3][:, CH - 1:CH]).then_inc(sem["state_saved"], 1)

                def copy_projected(C, v, j):
                    act.wait_ge(sem["b_full"], v)
                    act.copy(hi[:], slot[j][0:64, :]).then_inc(sem["split_hi"], 1)
                    act.copy(dts[C[1] % 2][:], slot[j][64:96, :]).then_inc(sem["dts_ready"], 1)

                def second_part(C):
                    act.wait_ge(sem["rest_ready"], C + 1)
                    act.copy(mid[:], rest[:]).then_inc(sem["split_mid"], 1)

                def add_bias(v, j, t, par):
                    act.wait_ge(sem["b_full"], v)
                    act.activation(raw[:], slot[j][:], ACT.Identity, bias=bdt[par][:, t:t + 1])\
                        .then_inc(sem["raw_ready"], 1)

                def exp_log(TT):
                    act.wait_ge(sem["clamped"], TT + 1)
                    act.activation(ex[:], clamp[:], ACT.Exp).then_inc(sem["exp_ready"], 1)
                    act.wait_ge(sem["exp_ready"], TT + 1)
                    act.activation(ln[:], ex[:], ACT.Ln, bias=1.0).then_inc(sem["log_ready"], 1)

                def copy_y(C0, T_):
                    j = (T_ + 1) % 2
                    act.wait_ge(sem["reduced"], C0 * STEPS + (T_ * NS + 2))
                    stores = sem["y_even"] if j == 0 else sem["y_odd"]
                    act.wait_ge(stores, C0 * (8 * TILES) + (8 * T_ + (8 if j == 0 else 16)))
                    act.copy(ybuf[j][:], psy[:]).then_inc(sem["y_copied"], 1)

                act.sem_inc(sem["c_copied"], 1)
                act.sem_inc(sem["state_saved"], 3)
                act.sem_inc(sem["y_even"], 16)
                act.sem_inc(sem["y_odd"], 32)
                copy_projected((0, 0), 1, 0)
                second_part(0)
                add_bias(2, 1, 0, 0)
                exp_log(0)
                decay_of(events[0], 0)
                per_g = NCH // BODY_CHUNKS
                with act.Fori(0, G) as g:
                    act.wait_ge(sem["h_ready"], g * (NCH * STEPS) + 2)
                    act.wait_ge(sem["state_saved"], g * (NCH * STEPS) + 3)
                    act.copy(state[:], T["zeros"][:, 0:TILES * NS]).then_inc(sem["state_zeroed"], 1)
                    with act.Fori(0, per_g) as half:
                        C0 = (g * per_g + half) * BODY_CHUNKS
                        act.activation(nothing[:], T["eps"][:], ACT.Ln)
                        for v, e in enumerate(events):
                            full = C0 * (NE // BODY_CHUNKS) + (v + 3)
                            if e[0] == "xdbl":
                                copy_projected((C0 + e[1], e[1]), full, v % 2)
                                continue
                            if e[0] == "delta":
                                add_bias(full, v % 2, e[2], e[1] % 2)
                                continue
                            _, q, t, n = e
                            w = v + 1
                            while events[w % NE][0] != "step":
                                w += 1
                            decay_of(events[w % NE], C0 + BODY_CHUNKS * (w // NE))
                            copy_c(e, C0)
                            if step_of(e) > 0:
                                u_ = v - 1
                                while events[u_][0] != "step":
                                    u_ -= 1
                                save(events[u_], C0)
                            if n == STORE_AT:
                                T_ = q * TILES + t
                                copy_y(C0, T_)
                            if t == TILES - 1 and n == XDBL_AFTER + 1:
                                second_part(C0 + (q + 1))
                            if n == DELTA_AFTER + 1:
                                exp_log(C0 * TILES + (q * TILES + t + 1))
                        save(events[NE - 1], C0)
                act.wait_ge(sem["c_full"], NC * STEPS + 1)
                act.wait_ge(sem["gated"], NC * STEPS + 3)
                act.sem_inc(sem["c_copied"], C_LAG - 1)
                copy_y(NC, 0)

            @block.gpsimd
            def _(pool):
                def gate(e, C0):
                    s = step_of(e)
                    S = C0 * STEPS + s
                    pool.wait_ge(sem["h_ready"], S + 3)
                    pool.wait_ge(sem["c_copied"], S + 2)
                    pool.wait_ge(sem["reduced"], S + 1)
                    pool.tensor_tensor(gh[s % 2][:], h[s % 3][:], csb[s % 2][:], ALU.mult).then_inc(sem["gated"], 1)

                def delta_u(C0, T_):
                    q, t = T_ // TILES, T_ % TILES
                    pool.wait_ge(sem["delta_ready"], C0 * TILES + (T_ + 1))
                    pool.wait_ge(sem["x_full"], (C0 + q) * 80 + 80)
                    pool.tensor_tensor(du[T_ % 2][:], delta[T_ % 2][:], u[q % 2][:, t, :], ALU.mult)\
                        .then_inc(sem["du_ready"], 1)

                pool.sem_inc(sem["gated"], 3)
                delta_u(0, 0)
                with pool.Fori(0, NC // BODY_CHUNKS) as i:
                    C0 = i * BODY_CHUNKS
                    for e in events:
                        if e[0] != "step":
                            continue
                        gate(e, C0)
                        if e[3] == DELTA_AFTER + 4:
                            delta_u(C0, e[1] * TILES + e[2] + 1)
        clear(nc, sem)


def merge_stage(nc, kind, T, W, useq, yseq, zgate, x_t, out, last):
    K = DIRS[kind]
    norm = kind != "causal"
    assert not (last and kind == "snake")
    names = ("w_in y_in y_used first_sum paired summed dsum x_in x_free gate_in0 gate_in1 centred_full "
             "squared var_full rooted inverted normed affine gated out_full out_free out_stored x_done "
             "x_stored")
    with ExitStack() as ctx:
        sem = stage_semaphores(nc, ctx, names)
        def sb(name, shape, dt=F32):
            return ctx.enter_context(nc.sbuf_tensor(name + W["tag"], shape, dt))
        yb = [sb(f"yb{k}", [P, L]) for k in range(K)]
        ub = sb("ub", [P, L])
        total = sb("total", [P, TILES, L])
        xr = sb("xr", [DM, 2, L])
        wo = sb("wo", [P, TILES * DM])
        ds = sb("ds", [P, TILES * K])
        dsum = sb("dsum", [P, TILES])
        lng, lnb = (sb(n, [P, TILES]) for n in ("lng", "lnb"))
        centre_by, average_by = (sb(n, [P, TILES, TILES, P]) for n in ("centre_by", "average_by"))
        zc = [sb(f"zc{j}", [P, TILES, BANK]) for j in range(2)]
        sq = sb("sq", [P, TILES, BANK])
        root = sb("root", [P, TILES, BANK])
        tn = sb("tn", [P, TILES, BANK])
        ob = sb("ob", [P, 2, 4, DM])
        cent = ctx.enter_context(nc.psum_tensor("cent" + W["tag"], [P, TILES, BANK], F32))
        varp = ctx.enter_context(nc.psum_tensor("varp" + W["tag"], [P, TILES, BANK], F32))
        outp = ctx.enter_context(nc.psum_tensor("outp" + W["tag"], [P, 2, BANK], F32))
        y_v = yseq.rearrange("(k p c) t q l -> k p c t q l", p=PAIRS, c=NCH)
        u_v = useq.rearrange("(k p c) t q l -> k p c t q l", p=PAIRS, c=NCH)
        NB = BANKS_L
        YPER = 16 * (K + 1)
        MATES = {0: (0, 1), 1: (0, 1, 2), 2: (1, 2)}

        def store_tokens(sp, p, c):
            sp.wait_ge(sem["x_done"], p * NB + (c + 1))
            for b in range(2):
                sp.dma_start(out[p * 2 + b, c * BANK:(c + 1) * BANK, :].rearrange("(j q) d -> q j d", q=P),
                             ob[:, b]).then_inc(sem["out_stored"], 16)

        def residual(dve, p, c):
            if last:
                return
            dve.wait_ge(sem["out_full"], p * NB + (c + 1))
            if c == 0:
                dve.wait_ge(sem["x_in"], p * 16 + 16)
            for b in range(2):
                img = xr[:, b, :].rearrange("q (h w) -> q h w", w=SIDE)
                src = outp[0:DM, b, :].rearrange("q (h w) -> q h w", w=SIDE)
                a = c * ROWS_PER_BANK
                for cols, view in first_order(kind, img, (a, a + ROWS_PER_BANK)):
                    ins = dve.tensor_tensor(view, view, src[:, :, cols], ALU.add)
            ins.then_inc(sem["x_done"], 1)

        with nc.Block() as block:
            @block.sync
            def _(sp):
                for dst, name in ((wo, "wo"), (ds, "ds"), (lng, "lng"), (lnb, "lnb"), (centre_by, "centre"),
                                  (average_by, "average")):
                    sp.dma_start(dst[:], W[name]).then_inc(sem["w_in"], 16)
                with sp.Fori(0, PAIRS) as p:
                    sp.wait_ge(sem["x_free"], p + 1)
                    sp.dma_start(xr[:], x_t[bass.ds(2 * p, 2)].rearrange("b c l -> c b l")).then_inc(sem["x_in"], 16)
                    for t in range(TILES):
                        sp.wait_ge(sem["y_used"], p * TILES + (t + 1))
                        for k in range(K):
                            sp.dma_start(yb[k][:].rearrange("q (c l) -> q c l", l=CH),
                                         y_v[k, p, :, t].rearrange("c q l -> q c l")).then_inc(sem["y_in"], 16)
                        sp.dma_start(ub[:].rearrange("q (c l) -> q c l", l=CH),
                                     u_v[0, p, :, t].rearrange("c q l -> q c l")).then_inc(sem["y_in"], 16)
                    for c in range(NB):
                        sp.wait_ge(sem["gated"], p * NB + (c + 1))
                        sp.dma_start(zc[c % 2][:], zgate[p, c].rearrange("t q l -> q t l"))\
                            .then_inc(sem["gate_in0"] if c % 2 == 0 else sem["gate_in1"], 16)
                        if last and c > 0:
                            store_tokens(sp, p, c - 1)
                    if last:
                        store_tokens(sp, p, NB - 1)
                    else:
                        sp.wait_ge(sem["x_done"], (p + 1) * NB)
                        sp.dma_start(x_t[bass.ds(2 * p, 2)].rearrange("b c l -> c b l"), xr[:]).then_inc(sem["x_stored"], 16)
                        sp.wait_ge(sem["x_stored"], p * 16 + 16)
                        sp.sem_inc(sem["x_free"], 1)
                if last:
                    sp.wait_ge(sem["out_stored"], 32 * PAIRS * NB + 32)
                else:
                    sp.wait_ge(sem["x_stored"], 16 * PAIRS)

            @block.tensor
            def _(pe):
                def mix(dst, src_of, mats, ready_inc):
                    for d in range(TILES):
                        for n, s in enumerate(MATES[d]):
                            mm = pe.matmul(dst[:, d, :], mats[:, s, d, :], src_of(s), start=(n == 0),
                                           stop=(n == len(MATES[d]) - 1))
                    mm.then_inc(ready_inc, 1)

                def centre(p, c, count):
                    pe.wait_ge(sem["normed"], count)
                    mix(cent, lambda s: total[:, s, c * BANK:(c + 1) * BANK], centre_by, sem["centred_full"])

                def project(p, c):
                    pe.wait_ge(sem["gated"], p * NB + (c + 3))
                    if last:
                        pe.wait_ge(sem["out_free"], p * NB + (c + 1))
                    elif c:
                        pe.wait_ge(sem["x_done"], p * NB + c)
                    for b in range(2):
                        half = slice(64 * b, 64 * b + 64)
                        if not last:
                            pe.matmul(outp[0:DM, b, :], wo[:, 2 * b * DM:(2 * b + 1) * DM], tn[:, 2 * b, :],
                                      start=True, stop=False)
                            mm = pe.matmul(outp[0:DM, b, :], wo[half, DM:2 * DM], tn[half, 1, :],
                                           start=False, stop=True)
                        else:
                            for j in range(4):
                                o = outp[:, b, j * DM:(j + 1) * DM]
                                tok = slice(j * P, (j + 1) * P)
                                pe.matmul(o, tn[:, 2 * b, tok], wo[:, 2 * b * DM:(2 * b + 1) * DM],
                                          start=True, stop=False)
                                pe.matmul(o, tn[half, 1, tok], wo[half, DM:2 * DM], start=False, stop=False)
                                mm = pe.matmul(o, xr[:, b, c * BANK + j * P:c * BANK + (j + 1) * P],
                                               T["ident"][0:DM, 0:DM], start=False, stop=True)
                    mm.then_inc(sem["out_full"], 1)

                pe.wait_ge(sem["w_in"], 96)
                with pe.Fori(0, PAIRS) as p:
                    pe.wait_ge(sem["summed"], (p + 1) * TILES)
                    pe.wait_ge(sem["x_in"], p * 16 + 16)
                    if norm:
                        centre(p, 0, p * NB + 1)
                    for c in range(NB):
                        if norm:
                            pe.wait_ge(sem["squared"], p * NB + (c + 1))
                            mix(varp, lambda s: sq[:, s, :], average_by, sem["var_full"])
                            if c + 1 < NB:
                                centre(p, c + 1, p * NB + (c + 2))
                        project(p, c)
                    if last:
                        pe.wait_ge(sem["out_full"], (p + 1) * NB)
                        pe.sem_inc(sem["x_free"], 1)

            @block.scalar
            def _(act):
                if not norm and not last:
                    return
                with act.Fori(0, PAIRS) as p:
                    for c in range(NB):
                        if norm:
                            act.wait_ge(sem["centred_full"], p * NB + (c + 1))
                            act.activation(sq[:], cent[:], ACT.Square).then_inc(sem["squared"], 1)
                            act.wait_ge(sem["var_full"], p * NB + (c + 1))
                            act.activation(root[:], varp[:], ACT.Sqrt, bias=T["eps"][:, 0:1]).then_inc(sem["rooted"], 1)
                            act.wait_ge(sem["normed"], p * NB + (c + 2))
                            for t in range(TILES):
                                act.activation(tn[:, t, :], tn[:, t, :], ACT.Identity, bias=lnb[:, t:t + 1],
                                               scale=lng[:, t:t + 1]).then_inc(sem["affine"], 1)
                        if last:
                            act.wait_ge(sem["out_full"], p * NB + (c + 1))
                            act.wait_ge(sem["out_stored"], p * (32 * NB) + 32 * (c + 1))
                            act.copy(ob[:].rearrange("q b j d -> q b (j d)"), outp[:, :, 0:4 * DM])\
                                .then_inc(sem["x_done"], 1)
                            act.wait_ge(sem["x_done"], p * NB + (c + 1))
                            act.sem_inc(sem["out_free"], 1)

            @block.vector
            def _(dve):
                dve.sem_inc(sem["x_free"], 1)
                dve.sem_inc(sem["y_used"], 1)
                dve.sem_inc(sem["normed"], 1)
                dve.sem_inc(sem["out_free"], 1)
                dve.sem_inc(sem["out_stored"], 32)
                dve.wait_ge(sem["w_in"], 96)
                dve.tensor_reduce(dsum[:], ds[:].rearrange("q (t k) -> q t k", k=K), mybir.AxisListType.X, ALU.add)\
                    .then_inc(sem["dsum"], 1)
                dve.wait_ge(sem["dsum"], 1)
                SUMS = 4 if kind == "snake" else 3 if K > 1 else 1
                with dve.Fori(0, PAIRS) as p:
                    dve.wait_ge(sem["gated"], p * NB + 2)
                    for t in range(TILES):
                        dve.wait_ge(sem["y_in"], p * (TILES * YPER) + (t + 1) * YPER)
                        acc = total[:, t, :]
                        n = p * (TILES * SUMS) + t * SUMS

                        def add(view, acc_view, i, done=False):
                            dve.wait_ge(sem["first_sum"], n + i)
                            dve.tensor_tensor(acc_view, acc_view, view, ALU.add).then_inc(sem["first_sum"], 1)

                        dve.scalar_tensor_tensor(out=acc, in0=ub[:], scalar=dsum[:, t:t + 1], in1=yb[0][:],
                                                 op0=ALU.mult, op1=ALU.add).then_inc(sem["first_sum"], 1)
                        if K > 1:
                            add(yb[2][:, ::-1], acc, 1)
                            dve.wait_ge(sem["paired"], p * TILES + (t + 1))
                            col = yb[1][:].rearrange("q (w h) -> q w h", h=SIDE)
                            img = acc.rearrange("q (h w) -> q h w", w=SIDE)
                            for i, (rows, view) in enumerate(column_order(kind, img)):
                                add(col[:, :, rows], view, 2 + i)
                        dve.wait_ge(sem["first_sum"], n + SUMS)
                        dve.sem_inc(sem["y_used"], 1)
                        dve.sem_inc(sem["summed"], 1)
                    for c in range(NB):
                        if norm:
                            dve.wait_ge(sem["rooted"], p * NB + (c + 1))
                            dve.reciprocal(root[:], root[:]).then_inc(sem["inverted"], 1)
                            dve.wait_ge(sem["inverted"], p * NB + (c + 1))
                            if c:
                                residual(dve, p, c - 1)
                            if c:
                                dve.wait_ge(sem["out_full"], p * NB + c)
                            else:
                                dve.wait_ge(sem["x_in"], p * 16 + 16)
                            dve.tensor_tensor(tn[:], cent[:], root[:], ALU.mult).then_inc(sem["normed"], 1)
                        elif c:
                            residual(dve, p, c - 1)
                    residual(dve, p, NB - 1)

            @block.gpsimd
            def _(pool):
                pool.sem_inc(sem["gated"], 2)
                with pool.Fori(0, PAIRS) as p:
                    if K > 1:
                        for t in range(TILES):
                            pool.wait_ge(sem["y_in"], p * (TILES * YPER) + (t + 1) * YPER)
                            pool.tensor_tensor(yb[1][:], yb[1][:], yb[3][:, ::-1], ALU.add).then_inc(sem["paired"], 1)
                    if not norm:
                        pool.wait_ge(sem["summed"], (p + 1) * TILES)
                    for c in range(NB):
                        g = sem["gate_in0"] if c % 2 == 0 else sem["gate_in1"]
                        pool.wait_ge(g, p * (8 * NB) + 16 * (c // 2 + 1))
                        if norm:
                            pool.wait_ge(sem["affine"], p * (TILES * NB) + TILES * (c + 1))
                            src = tn[:]
                        else:
                            if c:
                                pool.wait_ge(sem["out_full"], p * NB + c)
                            else:
                                pool.wait_ge(sem["x_in"], p * 16 + 16)
                            src = total[:, :, c * BANK:(c + 1) * BANK]
                        pool.tensor_tensor(tn[:], src, zc[c % 2][:], ALU.mult).then_inc(sem["gated"], 1)
        clear(nc, sem)


def build(nc, args, out, layers=(0, 1, 2, 3)):
    names = ("win", "convw", "convb", "wx", "wdt", "bdt", "a_log", "ds", "lng", "lnb", "wo")
    shared = {k: args[k] for k in ("pick", "centre", "average")}
    W = {n: {"tag": f"_{n}", **shared, **{k: args[f"{k}{n}"] for k in names}} for n in layers}
    x_t = nc.dram_tensor("x_t", [NBATCH, DM, L], F32, kind="Internal").ap()
    chunks = 4 * PAIRS * NCH
    useq = nc.dram_tensor("useq", [chunks, TILES, P, CH], F32, kind="Internal").ap()
    yseq = nc.dram_tensor("yseq", [chunks, TILES, P, CH], F32, kind="Internal").ap()
    zgate = nc.dram_tensor("zgate", [PAIRS, BANKS_L, TILES, P, BANK], F32, kind="Internal").ap()
    neg_a = {n: nc.dram_tensor(f"neg_a{n}", [DIRS[KINDS[n]], P, TILES * NS], F32, kind="Internal").ap()
             for n in layers}
    with ExitStack() as ctx:
        T = {}
        for name, shape, dt in (("ident", [P, P], F32), ("group", [DM, DM], F32),
                                ("eps", [P, 1], F32), ("zeros", [P, TILES * NS], F32)):
            T[name] = ctx.enter_context(nc.sbuf_tensor(f"t_{name}", shape, dt))
        loaded = ctx.enter_context(nc.semaphore("tables_in"))
        filled = ctx.enter_context(nc.semaphore("tables_filled"))
        with nc.Block() as block:
            @block.sync
            def _(sp):
                for name in ("ident", "group"):
                    sp.dma_start(T[name][:], args[name]).then_inc(loaded, 16)
                sp.wait_ge(loaded, 32)

            @block.vector
            def _(dve):
                dve.memset(T["eps"][:], LN_EPS).then_inc(filled, 1)
                dve.memset(T["zeros"][:], 0.0).then_inc(filled, 1)
                dve.wait_ge(filled, 2)
        setup_stage(nc, T, W, layers, neg_a)
        to_channels_stage(nc, T, args["x"], x_t)
        for n in layers:
            kind = KINDS[n]
            count = DIRS[kind] * PAIRS * NCH
            expand_stage(nc, kind, T, W[n], x_t, useq[0:count], zgate)
            scan_stage(nc, kind, T, W[n], useq[0:count], neg_a[n], yseq[0:count])
            merge_stage(nc, kind, T, W[n], useq[0:count], yseq[0:count], zgate, x_t, out, n == layers[-1])


def tiles(a):
    return np.stack([a[:P], np.concatenate([a[P:], a[P:]]), a[:P]], axis=1)


def constants():
    batch = np.stack([np.zeros(P), np.repeat([0, 1], 64), np.ones(P)], axis=1)
    same = (batch[:, :, None, None] == batch.T[None, None]).astype(np.float32)
    eye = np.zeros((P, TILES, TILES, P), np.float32)
    for t in range(TILES):
        eye[:, t, t] = np.eye(P)
    one = 0x3F80
    pick = np.zeros((3, 2, NS, TILES, NS, P), np.uint16)
    for b in range(2):
        for n in range(NS):
            pick[:, b, n, :, n] = one * (batch.T == b)
    group = np.kron(np.eye(DM // 3), np.ones((3, 3))) / 3
    return {
        "ident": np.eye(P, dtype=np.float32),
        "pick": pick.reshape(96, TILES, NS, P),
        "group": group.astype(np.float32),
        "average": (same / DI).astype(np.float32),
        "centre": (eye - same / DI).astype(np.float32),
    }


def layer_arrays(n, w):
    K = DIRS[KINDS[n]]
    xp, dt, db, al, dsk = w["xp"], w["dt"], w["db"], w["al"], w["ds"]
    R = dt.shape[2]
    wx = np.zeros((K, P, TILES, 96), np.float32)
    wdt = np.zeros((K, 32, TILES, P), np.float32)
    for b in range(2):
        rows = slice(64 * b, 64 * b + 64)
        for k in range(K):
            for cols, src in ((slice(NS * b, NS * b + NS), xp[k, R:R + NS]),
                              (slice(32 + NS * b, 32 + NS * b + NS), xp[k, R + NS:]),
                              (slice(64 + RMAX * b, 64 + RMAX * b + R), xp[k, :R])):
                wx[k, :, 2 * b, cols] = src[:, :P].T
                wx[k, rows, 1, cols] = src[:, P:].T
            r = slice(RMAX * b, RMAX * b + R)
            wdt[k, r, 2 * b, :] = dt[k, :P].T
            wdt[k, r, 1, rows] = dt[k, P:].T
    per_dir = lambda a: np.stack([tiles(a[k]) for k in range(K)])
    arrays = {
        "win": w["win"].T,
        "convw": tiles(w["cw"].reshape(DI, -1)).reshape(P, -1),
        "convb": tiles(w["cb"]),
        "wx": wx, "wdt": wdt, "bdt": per_dir(db),
        "a_log": per_dir(al.reshape(K, DI, NS)).transpose(1, 0, 2, 3).reshape(P, -1),
        "ds": tiles(dsk.reshape(K, DI).T).reshape(P, -1),
        "lng": tiles(w["lng"]), "lnb": tiles(w["lnb"]),
        "wo": tiles(w["wo"].T).reshape(P, -1),
    }
    return {f"{k}{n}": np.ascontiguousarray(v) for k, v in arrays.items()}


def layout(v, layers=(0, 1, 2, 3)):
    arrays = {"x": np.ascontiguousarray(v["x"]).reshape(NBATCH, L, DM), **constants()}
    keys = [
        dict(win="in_proj_w", cw="conv_w", cb="conv_b", xp="x_proj_w", dt="dt_proj_w", db="dt_proj_b", al="A_logs",
             ds="Ds", lng="ln_gamma", lnb="ln_beta", wo="out_proj_w"),
        dict(win="in_proj_w", cw="conv_w", cb="conv_b", xp="x_proj_weight", dt="dt_projs_weight",
             db="dt_projs_bias", al="A_logs", ds="Ds", lng="out_norm_w", lnb="out_norm_b", wo="out_proj_w"),
        dict(win="in_proj_w", cw="conv_w", cb="conv_b", xp="x_proj_w", dt="dt_projs_w", db="dt_projs_b",
             al="A_logs", ds="Ds", lng="ln_g", lnb="ln_b", wo="out_proj_w"),
        dict(win="W_in", cw="conv_w", cb="conv_b", xp="W_x", dt="W_dt", db="b_dt", al="A_log", ds="D",
             lng="D", lnb="D", wo="W_out"),
    ]
    for n in layers:
        w = {k: np.asarray(v[f"L{n}_conv_{name}"]) for k, name in keys[n].items()}
        if n == 3:
            w.update({k: w[k][None] for k in ("xp", "dt", "db")})
        arrays.update(layer_arrays(n, w))
    return arrays


def kernel(**inputs):
    import concourse.bacc as bacc
    from concourse.bass_utils import run_bass_kernel_spmd

    nc = bacc.Bacc("TRN2", target_bir_lowering=False, num_devices=1)
    arrays = layout(inputs)
    args = {k: nc.dram_tensor(f"in_{k}", a.shape, mybir.dt.from_np(a.dtype), kind="ExternalInput").ap()
            for k, a in arrays.items()}
    out = nc.dram_tensor("out", [NBATCH, L, DM], F32, kind="ExternalOutput").ap()
    build(nc, args, out)
    r = run_bass_kernel_spmd(nc, [{f"in_{k}": a for k, a in arrays.items()}], core_ids=[0])
    return r.results[0]["out"].reshape(NBATCH, SIDE, SIDE, DM)
```

```python
from contextlib import ExitStack

import numpy as np

import concourse.bass as bass
from concourse import mybir

F32 = mybir.dt.float32
BF16 = mybir.dt.bfloat16
ALU = mybir.AluOpType
ACT = mybir.ActivationFunctionType

P = 128
NBATCH, SIDE, DM = 8, 64, 96
L = SIDE * SIDE
DI = 2 * DM
NS = 16
RMAX = 16
PAIRS = NBATCH // 2
TILES = 3
BANK = 512
BANKS_L = L // BANK
ROWS_PER_BANK = BANK // SIDE
CH = 1024
HALVES = CH // BANK
NCH = L // CH
PAD = SIDE + 2
GN_EPS = LN_EPS = 1e-5

KINDS = ["cross", "snake", "cross", "causal"]
DIRS = {"cross": 4, "snake": 4, "causal": 1}
SEQS = {"cross": 2, "snake": 2, "causal": 1}

STEPS = TILES * NS
LAST_USE = (2, 1, 3)
LAG, C_LAG, AHEAD, RING = 6, 4, 2, 3
XDBL_AFTER = [(0, 9), (0, 12)]
DELTA_AFTER = [(1, 10), (1, 12), (2, 3)]
LOGS_AT = (2, 8)
FINISH_AT = 10
STORE_AT = 1


def first_order(kind, natural, rows=(0, SIDE)):
    a, b = rows
    if kind != "snake":
        return [(slice(0, SIDE), natural[:, a:b, :])]
    lo, hi = SIDE - 1 - a, SIDE - 1 - b
    flipped = natural[:, lo:(hi if hi >= 0 else None):-1, 1::2]
    return [(slice(0, None, 2), natural[:, a:b, 0::2]), (slice(1, None, 2), flipped)]


def column_order(kind, image):
    if kind != "snake":
        return [(slice(0, SIDE), image.rearrange("p h w -> p w h"))]
    return [(slice(0, None, 2), image[:, 0::2, :].rearrange("p h w -> p w h")),
            (slice(1, None, 2), image[:, 1::2, ::-1].rearrange("p h w -> p w h"))]


def stage_semaphores(nc, ctx, names):
    return {n: ctx.enter_context(nc.semaphore(n)) for n in names.split()}


def clear(nc, sem):
    for s in sem.values():
        nc.sync.sem_clear(s)
    nc.all_engine_barrier()


def to_channels_stage(nc, T, x_in, x_t):
    names = ("tokens_in transposed copied tokens_used stored")
    blocks = L // P
    with ExitStack() as ctx:
        sem = stage_semaphores(nc, ctx, names)
        tokens = ctx.enter_context(nc.sbuf_tensor("tokens", [P, blocks, DM], F32))
        chan = ctx.enter_context(nc.sbuf_tensor("chan", [DM, L], F32))
        ps = ctx.enter_context(nc.psum_tensor("ps_t", [P, 2, BANK], F32))
        with nc.Block() as block:
            @block.sync
            def _(sp):
                with sp.Fori(0, NBATCH) as b:
                    sp.wait_ge(sem["tokens_used"], b + 1)
                    sp.dma_start(tokens[:], x_in[b].rearrange("(q n) c -> q n c", q=P)).then_inc(sem["tokens_in"], 16)
                    sp.wait_ge(sem["copied"], b * BANKS_L + BANKS_L + 2)
                    sp.dma_start(x_t[b], chan[:]).then_inc(sem["stored"], 16)
                sp.wait_ge(sem["stored"], 16 * (NBATCH + 1))

            @block.tensor
            def _(pe):
                pe.sem_inc(sem["tokens_used"], 1)
                with pe.Fori(0, NBATCH) as b:
                    pe.wait_ge(sem["tokens_in"], b * 16 + 16)
                    for c in range(BANKS_L):
                        pe.wait_ge(sem["copied"], b * BANKS_L + (c + 1))
                        for j in range(4):
                            mm = pe.transpose(ps[0:DM, c % 2, j * P:(j + 1) * P], tokens[:, 4 * c + j, :],
                                              T["ident"][:, :])
                            if j == 3:
                                mm.then_inc(sem["transposed"], 1)
                    pe.wait_ge(sem["transposed"], b * BANKS_L + BANKS_L)
                    pe.sem_inc(sem["tokens_used"], 1)

            @block.scalar
            def _(act):
                act.sem_inc(sem["copied"], 2)
                act.sem_inc(sem["stored"], 16)
                with act.Fori(0, NBATCH) as b:
                    act.wait_ge(sem["stored"], b * 16 + 16)
                    for c in range(BANKS_L):
                        act.wait_ge(sem["transposed"], b * BANKS_L + (c + 1))
                        act.copy(chan[:].rearrange("d (q n) -> d n q", n=blocks)[:, 4 * c:4 * c + 4, :],
                                 ps[0:DM, c % 2, :].rearrange("d (n q) -> d n q", q=P)).then_inc(sem["copied"], 1)
        clear(nc, sem)


def setup_stage(nc, T, W, layers, neg_a):
    names = ("logs_in exp_done neg_done stored")
    with ExitStack() as ctx:
        sem = stage_semaphores(nc, ctx, names)
        cols = [DIRS[KINDS[n]] * TILES * NS for n in layers]
        logs = [ctx.enter_context(nc.sbuf_tensor(f"logs{n}", [P, c], F32)) for n, c in zip(layers, cols)]
        with nc.Block() as block:
            @block.sync
            def _(sp):
                for n, t in zip(layers, logs):
                    sp.dma_start(t[:], W[n]["a_log"]).then_inc(sem["logs_in"], 16)
                for i, (n, t) in enumerate(zip(layers, logs)):
                    sp.wait_ge(sem["neg_done"], i + 1)
                    sp.dma_start(neg_a[n].rearrange("k p c -> p k c"),
                                 t[:].rearrange("p (k c) -> p k c", c=TILES * NS)).then_inc(sem["stored"], 16)
                sp.wait_ge(sem["stored"], 16 * len(layers))

            @block.scalar
            def _(act):
                act.wait_ge(sem["logs_in"], 16 * len(layers))
                for t in logs:
                    act.activation(t[:], t[:], ACT.Exp).then_inc(sem["exp_done"], 1)

            @block.vector
            def _(dve):
                for i, t in enumerate(logs):
                    dve.wait_ge(sem["exp_done"], i + 1)
                    dve.tensor_scalar(t[:], t[:], -1.0, None, ALU.mult).then_inc(sem["neg_done"], 1)
        clear(nc, sem)


def expand_stage(nc, kind, T, W, x_t, useq, zgate):
    K = SEQS[kind]
    causal = kind == "causal"
    TAPS = 3 if causal else 9
    xp_shape = [P, L + 2] if causal else [P, PAD * PAD]
    DCH = 2 * BANKS_L + 2 + 5
    CONVS = TILES * TAPS
    names = ("w_in x_in stats stats_seen free_seen aggr group_ps centred sqrt_done scale_ready normed ps_full ps_free padded "
             "pad_full conv_step conv_free silu_done rotated z_full x_free seq_out small z_out")
    with ExitStack() as ctx:
        sem = stage_semaphores(nc, ctx, names)
        def sb(name, shape, dt=F32):
            return ctx.enter_context(nc.sbuf_tensor(name + W["tag"], shape, dt))
        win = sb("win", [DM, 2 * DI])
        convw = sb("convw", [P, TILES * TAPS])
        convb = sb("convb", [P, TILES])
        xn = sb("xn", [DM, 2, L])
        bn = sb("bn", [DM, 2, BANKS_L, 6])
        mv = sb("mv", [DM, 2, 2])
        gmean, dev, var, rstd, nbias = (sb(n, [DM, 2]) for n in ("gmean", "dev", "gvar", "grstd", "gnbias"))
        xp = [sb(f"xp{j}", xp_shape) for j in range(2)]
        acc = [sb(f"acc{j}", [P, L]) for j in range(2)]
        zb = sb("zb", [P, L])
        us = [sb(f"us{k}", [P, L]) for k in range(K)]
        ps = ctx.enter_context(nc.psum_tensor("ps_e" + W["tag"], [P, 4, BANK], F32))
        psg = ctx.enter_context(nc.psum_tensor("ps_g" + W["tag"], [P, BANK], F32))

        useq_v = useq.rearrange("(k p c) t q l -> k p c t q l", p=PAIRS, c=NCH)
        PER = TILES * 2 * BANKS_L

        def interior(t, c):
            if causal:
                return xp[t % 2][:, 2 + c * BANK:2 + (c + 1) * BANK]
            img = xp[t % 2][:].rearrange("p (h w) -> p h w", h=PAD)
            return img[:, 1 + c * ROWS_PER_BANK:1 + (c + 1) * ROWS_PER_BANK, 1:1 + SIDE]

        with nc.Block() as block:
            @block.sync
            def _(sp):
                sp.dma_start(win[:], W["win"]).then_inc(sem["w_in"], 16)
                sp.dma_start(convw[:], W["convw"]).then_inc(sem["w_in"], 16)
                sp.dma_start(convb[:], W["convb"]).then_inc(sem["w_in"], 16)

                def load_x(p):
                    sp.dma_start(xn[:], x_t[bass.ds(2 * p, 2)].rearrange("b c l -> c b l")).then_inc(sem["x_in"], 16)

                load_x(0)
                with sp.Fori(0, PAIRS) as p:
                    for t in range(TILES):
                        sp.wait_ge(sem["z_full"], p * TILES + (t + 1))
                        sp.dma_start(zgate[p, :, t].rearrange("c q l -> q c l"),
                                     zb[:].rearrange("q (c l) -> q c l", l=BANK)).then_inc(sem["z_out"], 16)
                        if t == TILES - 1:
                            sp.wait_ge(sem["x_free"], p + 1)
                            load_x((p + 1) % PAIRS)
                        sp.wait_ge(sem["silu_done"], p * TILES + (t + 3))
                        for k in range(K):
                            if k:
                                sp.wait_ge(sem["rotated"], p * (TILES * (K - 1)) + (t * (K - 1) + k))
                            sp.dma_start(useq_v[k, p, :, t].rearrange("c q l -> q c l"),
                                         us[k][:].rearrange("q (c l) -> q c l", l=CH)).then_inc(sem["seq_out"], 16)
                sp.wait_ge(sem["x_in"], 16 * (PAIRS + 1))
                sp.wait_ge(sem["z_out"], 16 * (PAIRS * TILES + 1))
                sp.wait_ge(sem["seq_out"], 16 * K * (PAIRS * TILES + 1))

            @block.tensor
            def _(pe):
                pe.wait_ge(sem["w_in"], 48)
                with pe.Fori(0, PAIRS) as p:
                    pe.wait_ge(sem["aggr"], p + 1)
                    pe.matmul(psg[0:DM, 0:2], T["group"][:, :], mv[:, :, 0], start=True, stop=True)\
                        .then_inc(sem["group_ps"], 1)
                    pe.wait_ge(sem["centred"], p + 1)
                    pe.matmul(psg[0:DM, 2:4], T["group"][:, :], var[:, :], start=True, stop=True)\
                        .then_inc(sem["group_ps"], 1)
                    pe.wait_ge(sem["normed"], p * 2 + 2)
                    m = 0
                    for t in range(TILES):
                        for which in range(2):
                            for c in range(BANKS_L):
                                cols = slice(c * BANK, (c + 1) * BANK)
                                pe.wait_ge(sem["ps_free"], p * PER + (m + 1))
                                o = which * DI
                                if t != 1:
                                    mm = pe.matmul(ps[:, m % 4, :], win[:, o:o + P], xn[:, t // 2, cols],
                                                   start=True, stop=True)
                                else:
                                    for b in range(2):
                                        mm = pe.matmul(ps[64 * b:64 * b + 64, m % 4, :], win[:, o + P:o + DI],
                                                       xn[:, b, cols], start=True, stop=True)
                                mm.then_inc(sem["ps_full"], 1)
                                m += 1
                    pe.wait_ge(sem["ps_full"], p * PER + PER)
                    pe.sem_inc(sem["x_free"], 1)

            @block.scalar
            def _(act):
                act.sem_inc(sem["ps_free"], 4)
                act.sem_inc(sem["silu_done"], 2)
                act.sem_inc(sem["z_out"], 16)
                act.sem_inc(sem["seq_out"], 16 * K)
                act.wait_ge(sem["w_in"], 48)
                act.wait_ge(sem["padded"], 2)
                with act.Fori(0, PAIRS) as p:
                    act.wait_ge(sem["small"], p * 5 + 4)
                    act.activation(rstd[:], rstd[:], ACT.Sqrt).then_inc(sem["sqrt_done"], 1)
                    act.wait_ge(sem["scale_ready"], p + 1)
                    for b in range(2):
                        act.activation(xn[:, b, :], xn[:, b, :], ACT.Identity, bias=nbias[:, b:b + 1],
                                       scale=rstd[:, b:b + 1]).then_inc(sem["normed"], 1)
                    m = 0

                    def take(t, which):
                        nonlocal m
                        for c in range(BANKS_L):
                            act.wait_ge(sem["ps_full"], p * PER + (m + 1))
                            if which == 0:
                                if c == 0:
                                    act.wait_ge(sem["conv_free"], p * TILES + LAST_USE[t])
                                src = ps[:, m % 4, :]
                                if not causal:
                                    src = src.rearrange("p (h w) -> p h w", w=SIDE)
                                ins = act.copy(interior(t, c), src)
                                ins.then_inc(sem["ps_free"], 1)
                            else:
                                if c == 0:
                                    act.wait_ge(sem["z_out"], p * (16 * TILES) + 16 * (t + 1))
                                img = ps[:, m % 4, :].rearrange("p (h w) -> p h w", w=SIDE)
                                dst = zb[:].rearrange("p (h w) -> p h w", w=SIDE)
                                a = c * ROWS_PER_BANK
                                if kind != "snake":
                                    parts = [(dst[:, a:a + ROWS_PER_BANK, :], img)]
                                else:
                                    lo = SIDE - 1 - a
                                    hi = lo - ROWS_PER_BANK
                                    parts = [(dst[:, a:a + ROWS_PER_BANK, 0::2], img[:, :, 0::2]),
                                             (dst[:, lo:(hi if hi >= 0 else None):-1, 1::2], img[:, :, 1::2])]
                                for d, s in parts:
                                    ins = act.activation(d, s, ACT.Silu)
                                ins.then_inc(sem["ps_free"], 1)
                            m += 1
                        act.wait_ge(sem["ps_free"], p * PER + (m + 4))
                        act.sem_inc(sem["pad_full"] if which == 0 else sem["z_full"], 1)

                    def first_sequence(t):
                        act.wait_ge(sem["conv_step"], p * CONVS + (t + 1) * TAPS)
                        act.wait_ge(sem["seq_out"], p * (16 * K * TILES) + 16 * K * (t + 1))
                        src = acc[t % 2][:].rearrange("p (h w) -> p h w", w=SIDE)
                        dst = us[0][:].rearrange("p (h w) -> p h w", w=SIDE)
                        parts = first_order(kind, src)
                        for j, (cols, view) in enumerate(parts):
                            ins = act.activation(dst[:, :, cols], view, ACT.Silu, bias=convb[:, t:t + 1])
                        ins.then_inc(sem["silu_done"], 1)

                    take(0, 0)
                    take(0, 1)
                    take(1, 0)
                    take(1, 1)
                    first_sequence(0)
                    take(2, 0)
                    take(2, 1)
                    first_sequence(1)
                    first_sequence(2)

            @block.vector
            def _(dve):
                for j in range(2):
                    dve.memset(xp[j][:], 0.0).then_inc(sem["padded"], 1)
                dve.sem_inc(sem["conv_free"], 2)
                dve.wait_ge(sem["padded"], 2)
                dve.wait_ge(sem["w_in"], 48)
                with dve.Fori(0, PAIRS) as p:
                    dve.wait_ge(sem["x_in"], p * 16 + 16)
                    for b in range(2):
                        for c in range(BANKS_L):
                            dve.bn_stats(bn[:, b, c, :], xn[:, b, c * BANK:(c + 1) * BANK]).then_inc(sem["stats"], 1)
                    dve.wait_ge(sem["stats"], p * (2 * BANKS_L) + 2 * BANKS_L)
                    dve.sem_inc(sem["stats_seen"], 1)
                    dve.bn_aggr(mv[:, 0, :], bn[:, 0].rearrange("p c s -> p (c s)"))
                    dve.bn_aggr(mv[:, 1, :], bn[:, 1].rearrange("p c s -> p (c s)")).then_inc(sem["aggr"], 1)
                    dve.wait_ge(sem["group_ps"], p * 2 + 1)
                    dve.tensor_copy(gmean[:], psg[0:DM, 0:2]).then_inc(sem["small"], 1)
                    dve.wait_ge(sem["small"], p * 5 + 1)
                    dve.tensor_tensor(dev[:], mv[:, :, 0], gmean[:], ALU.subtract).then_inc(sem["small"], 1)
                    dve.wait_ge(sem["small"], p * 5 + 2)
                    dve.tensor_tensor(dev[:], dev[:], dev[:], ALU.mult).then_inc(sem["small"], 1)
                    dve.wait_ge(sem["small"], p * 5 + 3)
                    dve.tensor_tensor(var[:], dev[:], mv[:, :, 1], ALU.add).then_inc(sem["centred"], 1)
                    dve.wait_ge(sem["group_ps"], p * 2 + 2)
                    dve.tensor_scalar(rstd[:], psg[0:DM, 2:4], GN_EPS, None, ALU.add).then_inc(sem["small"], 1)
                    dve.wait_ge(sem["sqrt_done"], p + 1)
                    dve.reciprocal(rstd[:], rstd[:]).then_inc(sem["small"], 1)
                    dve.wait_ge(sem["small"], p * 5 + 5)
                    dve.scalar_tensor_tensor(out=nbias[:], in0=gmean[:], scalar=-1.0, in1=rstd[:], op0=ALU.mult,
                                             op1=ALU.mult).then_inc(sem["scale_ready"], 1)
                    for t in range(TILES):
                        dve.wait_ge(sem["pad_full"], p * TILES + (t + 1))
                        dve.wait_ge(sem["silu_done"], p * TILES + LAST_USE[t])
                        a = acc[t % 2][:] if causal else acc[t % 2][:].rearrange("p (h w) -> p h w", w=SIDE)
                        for tap in range(TAPS):
                            if causal:
                                src = xp[t % 2][:, tap:tap + L]
                            else:
                                dy, dx = tap // 3, tap % 3
                                src = xp[t % 2][:].rearrange("p (h w) -> p h w", h=PAD)[:, dy:dy + SIDE, dx:dx + SIDE]
                            w = convw[:, t * TAPS + tap:t * TAPS + tap + 1]
                            if tap == 0:
                                dve.tensor_scalar(a, src, w, None, ALU.mult).then_inc(sem["conv_step"], 1)
                            else:
                                dve.wait_ge(sem["conv_step"], p * CONVS + (t * TAPS + tap))
                                dve.scalar_tensor_tensor(out=a, in0=src, scalar=w, in1=a, op0=ALU.mult,
                                                         op1=ALU.add).then_inc(sem["conv_step"], 1)
                        dve.wait_ge(sem["conv_step"], p * CONVS + (t + 1) * TAPS)
                        dve.sem_inc(sem["conv_free"], 1)

            @block.gpsimd
            def _(pool):
                if K == 1:
                    return
                with pool.Fori(0, PAIRS) as p:
                    for t in range(TILES):
                        pool.wait_ge(sem["silu_done"], p * TILES + (t + 3))
                        pool.wait_ge(sem["seq_out"], p * (16 * K * TILES) + 16 * K * (t + 1))
                        pool.sem_inc(sem["free_seen"], 1)
                        img = us[0][:].rearrange("p (h w) -> p h w", w=SIDE)
                        col = us[1][:].rearrange("p (w h) -> p w h", h=SIDE)
                        for rows, view in column_order(kind, img):
                            ins = pool.tensor_copy(col[:, :, rows], view)
                        ins.then_inc(sem["rotated"], 1)
        clear(nc, sem)


def scan_stage(nc, kind, T, W, useq, neg_a, yseq):
    K = DIRS[kind]
    both_ways = K > 1
    G = SEQS[kind] * PAIRS
    NC = K * PAIRS * NCH
    BODY_CHUNKS = 2

    events = []
    for q in range(BODY_CHUNKS):
        for t in range(TILES):
            for n in range(NS):
                events.append(("step", q, t, n))
                if (t, n) in XDBL_AFTER:
                    events.append(("xdbl", q + 1, XDBL_AFTER.index((t, n)), 0))
                if (t, n) in DELTA_AFTER:
                    events.append(("delta", q + 1, DELTA_AFTER.index((t, n)), 0))
    NE = len(events)
    EC = NE // BODY_CHUNKS
    PRE = HALVES + TILES
    step_at = [v for v, e in enumerate(events) if e[0] == "step"]
    BS = len(step_at)

    def step_of(e):
        return e[1] * STEPS + e[2] * NS + e[3]

    def projections_after(s):
        return range(step_at[s] + 1, step_at[s + 1]) if s + 1 < len(step_at) else ()

    def ahead(s, k, C0):
        v = step_at[(s + k) % BS]
        return events[v], C0 + BODY_CHUNKS * ((s + k) // BS), v

    names = ("pick_in x_full b_full c_full b_multiplied c_copied decay_ready h_ready state_saved "
             "state_zeroed gated reduced raw_ready clamped exp_ready log_ready excess_step final_step "
             "delta_ready du_ready split_hi dts_ready rest_ready split_mid split_lo stacked y_copied "
             "y_even y_odd zeroed")
    with ExitStack() as ctx:
        sem = stage_semaphores(nc, ctx, names)
        def sb(name, shape, dt=F32):
            return ctx.enter_context(nc.sbuf_tensor(name + W["tag"], shape, dt))

        def ring(name, n, shape=(P, CH), dt=F32):
            return [sb(f"{name}{j}", list(shape), dt) for j in range(n)]
        pick = sb("pick", [96, TILES, NS, P], BF16)
        u, wx, wdt = ring("u", 2, (P, TILES, CH)), ring("wx", 2, (P, TILES, 96)), ring("wdt", 2, (32, TILES, P))
        bdt, na, bc = ring("bdt", 2, (P, TILES)), ring("na", 2, (P, TILES * NS)), ring("bc", 2, (96, 2, CH), BF16)
        hi, mid, lo = (sb(n, [64, CH], BF16) for n in ("hi", "mid", "lo"))
        rest = sb("rest", [64, CH])
        dts = ring("dts", 2, (32, CH))
        raw, ex, one = ring("raw", TILES), ring("ex", TILES), ring("one", TILES)
        delta, du, ybuf = ring("delta", 2), ring("du", 2), ring("ybuf", 2)
        decay, dbu, h, csb, gh = (ring(n, RING) for n in ("decay", "dbu", "h", "csb", "gh"))
        state = sb("state", [P, 2, TILES * NS])
        slot = [ctx.enter_context(nc.psum_tensor(f"slot{j}" + W["tag"], [P, CH], F32)) for j in range(2)]
        psc = ctx.enter_context(nc.psum_tensor("psc" + W["tag"], [P, CH], F32))
        psy = ctx.enter_context(nc.psum_tensor("psy" + W["tag"], [P, CH], F32))

        HALF = [slice(a * BANK, (a + 1) * BANK) for a in range(HALVES)]


        def backward(q):
            return both_ways and q % 2 == 1

        def chunk_and_direction(i, q):
            if not both_ways:
                return i * BODY_CHUNKS + q, (i * BODY_CHUNKS + q) // (PAIRS * NCH)
            if not backward(q):
                return i, i // (PAIRS * NCH)
            return (i // NCH) * NCH + ((i % NCH) * -1 + (NCH - 1)), i // (PAIRS * NCH) + SEQS[kind]

        with nc.Block() as block:
            @block.sync
            def _(sp):
                def load(i, q):
                    j = q
                    C, k = chunk_and_direction(i, q)
                    sp.dma_start(u[j][:], useq[C].rearrange("t q l -> q t l")).then_inc(sem["x_full"], 16)
                    sp.dma_start(wx[j][:], W["wx"][k]).then_inc(sem["x_full"], 16)
                    sp.dma_start(wdt[j][:], W["wdt"][k]).then_inc(sem["x_full"], 16)
                    sp.dma_start(bdt[j][:], W["bdt"][k]).then_inc(sem["x_full"], 16)
                    sp.dma_start(na[j][:], neg_a[k]).then_inc(sem["x_full"], 16)

                def stack(C, j):
                    for n, (part, ready) in enumerate([(hi, sem["split_hi"]), (mid, sem["split_mid"]), (lo, sem["split_lo"])]):
                        sp.wait_ge(ready, C * HALVES + HALVES)
                        for s in range(2):
                            sp.dma_start(bc[j][32 * n:32 * n + 32, s, :], part[32 * s:32 * s + 32, :])\
                                .then_inc(sem["stacked"], 16)

                load(0, 0)
                sp.dma_start(pick[:], W["pick"].bitcast(BF16)).then_inc(sem["pick_in"], 16)
                stack(0, 0)
                with sp.Fori(0, NC // BODY_CHUNKS) as i:
                    for q in range(BODY_CHUNKS):
                        C = i * BODY_CHUNKS + q
                        sp.wait_ge(sem["h_ready"], C * STEPS + RING)
                        if q + 1 < BODY_CHUNKS:
                            load(i, q + 1)
                        else:
                            load((i + 1) % (NC // BODY_CHUNKS), 0)
                        for t in range(TILES):
                            if t == TILES - 1:
                                stack(C + 1, (q + 1) % 2)
                            sp.wait_ge(sem["y_copied"], C * TILES + (t + 2))
                            j = (q * TILES + t) % 2
                            here = chunk_and_direction(i, q)[0]
                            if backward(q):
                                here = here + SEQS[kind] * PAIRS * NCH
                            sp.dma_start(yseq[here, t], ybuf[j][:]).then_inc(sem["y_even"] if j == 0 else sem["y_odd"], 16)
                sp.wait_ge(sem["y_even"], 8 * NC * TILES + 16)
                sp.wait_ge(sem["y_odd"], 8 * NC * TILES + 32)
                sp.wait_ge(sem["x_full"], 80 * (NC + 1))
                sp.wait_ge(sem["stacked"], 96 * (NC + 1))

            @block.tensor
            def _(pe):
                def fill_b(e, C0, v, first=False):
                    what, q, t, n = e
                    k = step_of(e)
                    if t == 0 and n == 0:
                        pe.wait_ge(sem["stacked"], C0 * 96 + 96 * (q + 1))
                    if not first or k >= 2:
                        pe.wait_ge(sem["b_multiplied"], C0 * STEPS + (k - 1))
                    for cols in HALF:
                        mm = pe.matmul(slot[k % 2][:, cols], pick[:, t, n, :], bc[q % 2][:, 0, cols],
                                       start=True, stop=True)
                    mm.then_inc(sem["b_full"], 1)

                def wait_emptied(e, C0):
                    what, q, t, n = e
                    if what == "step":
                        pe.wait_ge(sem["c_copied"], C0 * STEPS + (step_of(e) + 2))
                    elif what == "delta":
                        pe.wait_ge(sem["raw_ready"], C0 * TILES + (q * TILES + t + 1))
                    else:
                        pe.wait_ge(sem["dts_ready"], C0 * HALVES + (q * HALVES + t + 1))
                        pe.wait_ge(sem["rest_ready"], C0 * HALVES + (q * HALVES + t + 1))

                def fill_c(e, C0):
                    what, q, t, n = e
                    if what == "xdbl":
                        pe.wait_ge(sem["x_full"], C0 * 80 + 80 * (q + 1))
                        for s in range(TILES):
                            mm = pe.matmul(psc[0:96, HALF[t]], wx[q % 2][:, s, :], u[q % 2][:, s, HALF[t]],
                                           start=(s == 0), stop=(s == TILES - 1))
                    elif what == "delta":
                        pe.wait_ge(sem["dts_ready"], C0 * HALVES + HALVES * (q + 1))
                        for cols in HALF:
                            mm = pe.matmul(psc[:, cols], wdt[q % 2][:, t, :], dts[q % 2][:, cols],
                                           start=True, stop=True)
                    else:
                        if t == 0 and n == 0:
                            pe.wait_ge(sem["stacked"], C0 * 96 + 96 * (q + 1))
                        for cols in HALF:
                            mm = pe.matmul(psc[:, cols], pick[:, t, n, :], bc[q % 2][:, 1, cols],
                                           start=True, stop=True)
                    mm.then_inc(sem["c_full"], 1)

                def reduce(e, C0):
                    what, q, t, n = e
                    s = step_of(e)
                    pe.wait_ge(sem["gated"], C0 * STEPS + (s + 1 + RING))
                    if n == 0:
                        pe.wait_ge(sem["y_copied"], C0 * TILES + (q * TILES + t + 1))
                    for cols in HALF:
                        mm = pe.matmul(psy[:, cols], T["ident"][:, :], gh[s % RING][:, cols],
                                       start=(n == 0), stop=(n == NS - 1), skip_group_check=True)
                    mm.then_inc(sem["reduced"], 1)

                pe.wait_ge(sem["zeroed"], 1)
                for cols in HALF:
                    mm = pe.matmul(psy[:, cols], T["ident"][:, :], gh[0][:, cols], start=True, stop=True)
                mm.then_inc(sem["reduced"], RING)
                pre = [("xdbl", 0, a, 0) for a in range(HALVES)] + [("delta", 0, t, 0) for t in range(TILES)]
                pe.wait_ge(sem["pick_in"], 16)
                for j, e in enumerate(pre):
                    if j:
                        wait_emptied(pre[j - 1], 0)
                    fill_c(e, 0)
                for k in range(LAG):
                    fill_b(events[step_at[k]], 0, step_at[k], first=True)
                    if k < C_LAG:
                        wait_emptied((pre + events)[PRE + k - 1], 0)
                        fill_c(events[k], 0)
                with pe.Fori(0, NC // BODY_CHUNKS) as i:
                    C0 = i * BODY_CHUNKS
                    for v, e in enumerate(events):
                        if e[0] == "step":
                            reduce(e, C0)
                        w = v + C_LAG
                        wait_emptied(events[(w - 1) % NE], C0 + BODY_CHUNKS * ((w - 1) // NE))
                        fill_c(events[w % NE], C0 + BODY_CHUNKS * (w // NE))
                        if e[0] == "step":
                            fill_b(*ahead(step_of(e), LAG, C0))

            @block.vector
            def _(dve):
                def multiply(e, C0, v):
                    what, q, t, n = e
                    s = step_of(e)
                    T_ = q * TILES + t
                    dve.wait_ge(sem["b_full"], C0 * STEPS + (s + 1))
                    if n == 0:
                        dve.wait_ge(sem["du_ready"], C0 * TILES + (T_ + 1))
                    dve.wait_ge(sem["h_ready"], C0 * STEPS + (s + 1))
                    dve.tensor_tensor(dbu[s % RING][:], du[T_ % 2][:], slot[s % 2][:], ALU.mult)\
                        .then_inc(sem["b_multiplied"], 1)

                def scan(e, C0, g):
                    what, q, t, n = e
                    s = step_of(e)
                    S = C0 * STEPS
                    dve.wait_ge(sem["decay_ready"], S + (s + 1))
                    dve.wait_ge(sem["b_multiplied"], S + (s + 1))
                    dve.wait_ge(sem["gated"], S + (s + 1))
                    dve.wait_ge(sem["state_saved"], S + (s + 1))
                    if q == 0 and t == 0 and n == 0:
                        dve.wait_ge(sem["state_zeroed"], g + 1)
                    k = t * NS + n
                    order = slice(None, None, -1) if backward(q) else slice(None)
                    first = state[:, q if both_ways else 0, k:k + 1]
                    dve.tensor_tensor_scan(h[s % RING][:, order], decay[s % RING][:, order], dbu[s % RING][:, order],
                                           first, ALU.mult, ALU.add).then_inc(sem["h_ready"], 1)

                def remainder(H0, a, v):
                    dve.wait_ge(sem["split_hi"], H0 + 1)
                    dve.tensor_tensor(rest[:, HALF[a]], psc[0:64, HALF[a]], hi[:, HALF[a]], ALU.subtract)\
                        .then_inc(sem["rest_ready"], 1)

                def last_part(H0, a):
                    dve.wait_ge(sem["split_mid"], H0 + 1)
                    dve.tensor_tensor(lo[:, HALF[a]], rest[:, HALF[a]], mid[:, HALF[a]], ALU.subtract)\
                        .then_inc(sem["split_lo"], 1)

                def clamp(TT, t):
                    dve.wait_ge(sem["raw_ready"], TT + 1)
                    dve.tensor_scalar(ex[t][:], raw[t][:], 30.0, None, ALU.min).then_inc(sem["clamped"], 1)

                def one_plus(TT, t):
                    dve.wait_ge(sem["exp_ready"], TT + 1)
                    dve.tensor_scalar(one[t][:], ex[t][:], 1.0, 1.0, ALU.min, ALU.add).then_inc(sem["excess_step"], 1)

                def rounded(TT, t):
                    dve.wait_ge(sem["excess_step"], TT * 2 + 1)
                    dve.scalar_tensor_tensor(out=one[t][:], in0=one[t][:], scalar=1.0, in1=ex[t][:],
                                             op0=ALU.subtract, op1=ALU.subtract).then_inc(sem["excess_step"], 1)

                def log_corrected(TT, t):
                    dve.wait_ge(sem["log_ready"], TT + 1)
                    dve.wait_ge(sem["excess_step"], TT * 2 + 2)
                    dve.scalar_tensor_tensor(out=one[t][:], in0=one[t][:], scalar=-1.2e-7, in1=ex[t][:],
                                             op0=ALU.max, op1=ALU.subtract).then_inc(sem["final_step"], 1)

                def softplus(TT, T_):
                    t = T_ % TILES
                    dve.wait_ge(sem["final_step"], TT + 1)
                    dve.scalar_tensor_tensor(out=delta[T_ % 2][:], in0=one[t][:], scalar=-1.0, in1=raw[t][:],
                                             op0=ALU.mult, op1=ALU.max).then_inc(sem["delta_ready"], 1)

                dve.sem_inc(sem["h_ready"], RING)
                dve.memset(gh[0][:], 0.0).then_inc(sem["zeroed"], 1)
                for a in range(HALVES):
                    remainder(a, a, a - PRE)
                    last_part(a, a)
                for t in range(TILES):
                    clamp(t, t)
                    one_plus(t, t)
                    rounded(t, t)
                log_corrected(0, 0)
                softplus(0, 0)
                for k in range(AHEAD):
                    multiply(events[step_at[k]], 0, step_at[k])
                per_g = (2 if both_ways else 1) * NCH // BODY_CHUNKS
                with dve.Fori(0, G) as g:
                    with dve.Fori(0, per_g) as half:
                        C0 = (g * per_g + half) * BODY_CHUNKS
                        for s, v in enumerate(step_at):
                            e = events[v]
                            what, q, t, n = e
                            multiply(*ahead(s, AHEAD, C0))
                            for w in projections_after(s):
                                if events[w][0] == "xdbl":
                                    remainder(C0 * HALVES + (events[w][1] * HALVES + events[w][2]), events[w][2], w)
                            scan(e, C0, g)
                            for w in projections_after(s):
                                if events[w][0] == "delta":
                                    clamp(C0 * TILES + (events[w][1] * TILES + events[w][2]), events[w][2])
                            for a in range(HALVES):
                                if (t, n - 2) == XDBL_AFTER[a]:
                                    last_part(C0 * HALVES + ((q + 1) * HALVES + a), a)
                            for d in range(TILES):
                                if (t, n - 2) == DELTA_AFTER[d]:
                                    one_plus(C0 * TILES + ((q + 1) * TILES + d), d)
                                if (t, n - 3) == DELTA_AFTER[d]:
                                    rounded(C0 * TILES + ((q + 1) * TILES + d), d)
                            T_ = q * TILES + t + 1
                            if n == FINISH_AT:
                                log_corrected(C0 * TILES + T_, T_ % TILES)
                            if n == FINISH_AT + 1:
                                softplus(C0 * TILES + T_, T_)
                dve.wait_ge(sem["b_full"], NC * STEPS + AHEAD + 2)
                dve.sem_inc(sem["b_multiplied"], LAG - AHEAD - 2)

            @block.scalar
            def _(act):
                def decay_of(e, C0, v):
                    what, q, t, n = e
                    s = step_of(e)
                    if n == 0:
                        act.wait_ge(sem["delta_ready"], C0 * TILES + (q * TILES + t + 1))
                    act.wait_ge(sem["h_ready"], C0 * STEPS + (s + 1))
                    k = t * NS + n
                    act.activation(decay[s % RING][:], delta[(q * TILES + t) % 2][:], ACT.Exp,
                                   scale=na[q % 2][:, k:k + 1]).then_inc(sem["decay_ready"], 1)

                def copy_c(e, C0, v):
                    s = step_of(e)
                    act.wait_ge(sem["c_full"], C0 * EC + (v + 1 + PRE))
                    act.wait_ge(sem["gated"], C0 * STEPS + (s + 1))
                    act.copy(csb[s % RING][:], psc[:]).then_inc(sem["c_copied"], 1)

                def save(s, C0):
                    k = s % STEPS
                    act.wait_ge(sem["h_ready"], C0 * STEPS + (s + 1 + RING))
                    q = s // STEPS
                    end = slice(0, 1) if backward(q) else slice(CH - 1, CH)
                    act.copy(state[:, q if both_ways else 0, k:k + 1], h[s % RING][:, end])\
                        .then_inc(sem["state_saved"], 1)

                def copy_projected(C0, q, a, v):
                    act.wait_ge(sem["c_full"], C0 * EC + (v + 1 + PRE))
                    act.copy(hi[:, HALF[a]], psc[0:64, HALF[a]]).then_inc(sem["split_hi"], 1)
                    act.copy(dts[q % 2][:, HALF[a]], psc[64:96, HALF[a]]).then_inc(sem["dts_ready"], 1)

                def second_part(H0, a):
                    act.wait_ge(sem["rest_ready"], H0 + 1)
                    act.copy(mid[:, HALF[a]], rest[:, HALF[a]]).then_inc(sem["split_mid"], 1)

                def add_bias(C0, q, t, v):
                    act.wait_ge(sem["c_full"], C0 * EC + (v + 1 + PRE))
                    act.activation(raw[t][:], psc[:], ACT.Identity, bias=bdt[q % 2][:, t:t + 1])\
                        .then_inc(sem["raw_ready"], 1)

                def exponential(TT, t):
                    act.wait_ge(sem["clamped"], TT + 1)
                    act.activation(ex[t][:], ex[t][:], ACT.Exp).then_inc(sem["exp_ready"], 1)

                def logarithm(TT, t):
                    act.wait_ge(sem["excess_step"], TT * 2 + 2)
                    act.activation(ex[t][:], ex[t][:], ACT.Ln, bias=1.0).then_inc(sem["log_ready"], 1)

                def copy_y(C0, T_):
                    j = (T_ + 1) % 2
                    act.wait_ge(sem["reduced"], C0 * STEPS + (T_ * NS + RING))
                    stores = sem["y_even"] if j == 0 else sem["y_odd"]
                    act.wait_ge(stores, C0 * (8 * TILES) + (8 * T_ + (8 if j == 0 else 16)))
                    act.copy(ybuf[j][:], psy[:]).then_inc(sem["y_copied"], 1)

                act.sem_inc(sem["c_copied"], 1)
                act.sem_inc(sem["state_saved"], RING)
                act.sem_inc(sem["y_even"], 16)
                act.sem_inc(sem["y_odd"], 32)
                for a in range(HALVES):
                    copy_projected(0, 0, a, a - PRE)
                    second_part(a, a)
                for t in range(TILES):
                    add_bias(0, 0, t, HALVES + t - PRE)
                    exponential(t, t)
                for t in range(TILES):
                    logarithm(t, t)
                for k in range(AHEAD):
                    decay_of(events[step_at[k]], 0, 0)
                copy_c(events[0], 0, 0)
                per_g = (2 if both_ways else 1) * NCH // BODY_CHUNKS
                with act.Fori(0, G) as g:
                    act.wait_ge(sem["h_ready"], g * (per_g * BS) + RING)
                    act.wait_ge(sem["state_saved"], g * (per_g * BS) + RING)
                    act.copy(state[:].rearrange("p a k -> p (a k)"), T["zeros"][:, :]).then_inc(sem["state_zeroed"], 1)
                    with act.Fori(0, per_g) as half:
                        C0 = (g * per_g + half) * BODY_CHUNKS
                        for s, v in enumerate(step_at):
                            what, q, t, n = events[v]
                            for w in projections_after(s):
                                if events[w][0] == "xdbl":
                                    copy_projected(C0, events[w][1], events[w][2], w)
                                else:
                                    add_bias(C0, events[w][1], events[w][2], w)
                            copy_c(*ahead(s, 1, C0))
                            decay_of(*ahead(s, AHEAD, C0))
                            if s > 0:
                                save(s - 1, C0)
                            if n == STORE_AT:
                                copy_y(C0, q * TILES + t)
                            for a in range(HALVES):
                                if (t, n - 1) == XDBL_AFTER[a]:
                                    second_part(C0 * HALVES + ((q + 1) * HALVES + a), a)
                            for d in range(TILES):
                                if (t, n - 1) == DELTA_AFTER[d]:
                                    exponential(C0 * TILES + ((q + 1) * TILES + d), d)
                            if (t, n) == LOGS_AT:
                                for d in range(TILES):
                                    logarithm(C0 * TILES + ((q + 1) * TILES + d), d)
                        save(BS - 1, C0)
                act.wait_ge(sem["c_full"], NC * EC + PRE + 2)
                act.wait_ge(sem["gated"], NC * STEPS + RING)
                act.sem_inc(sem["c_copied"], C_LAG - 2)
                copy_y(NC, 0)

            @block.gpsimd
            def _(pool):
                def gate(e, C0):
                    s = step_of(e)
                    S = C0 * STEPS
                    pool.wait_ge(sem["h_ready"], S + (s + 1 + RING))
                    pool.wait_ge(sem["c_copied"], S + (s + 2))
                    pool.wait_ge(sem["reduced"], S + (s + 1))
                    pool.tensor_tensor(gh[s % RING][:], h[s % RING][:], csb[s % RING][:], ALU.mult)\
                        .then_inc(sem["gated"], 1)

                def delta_u(C0, T_):
                    q, t = T_ // TILES, T_ % TILES
                    pool.wait_ge(sem["delta_ready"], C0 * TILES + (T_ + 1))
                    pool.wait_ge(sem["x_full"], C0 * 80 + 80 * (q + 1))
                    pool.tensor_tensor(du[T_ % 2][:], delta[T_ % 2][:], u[q % 2][:, t, :], ALU.mult)\
                        .then_inc(sem["du_ready"], 1)

                pool.sem_inc(sem["gated"], RING)
                delta_u(0, 0)
                with pool.Fori(0, NC // BODY_CHUNKS) as i:
                    C0 = i * BODY_CHUNKS
                    for e in events:
                        if e[0] != "step":
                            continue
                        gate(e, C0)
                        if e[3] == FINISH_AT + 2:
                            delta_u(C0, e[1] * TILES + e[2] + 1)
        clear(nc, sem)


def merge_stage(nc, kind, T, W, useq, yseq, zgate, x_t, out, last):
    K = DIRS[kind]
    norm = kind != "causal"
    assert not (last and norm)
    names = ("w_in job_in0 job_in1 job_in2 paired total_step dsum x_in x_free gate_in0 gate_in1 "
             "centred_full squared copied var_full rooted inverted spread normed affine gated "
             "out_full out_stored x_done x_stored")
    NB = BANKS_L
    DEPTH = 3
    jobs = [(w, t, c) for t in range(TILES) for w in (("row", "col") if K > 1 else ("row",)) for c in range(NCH)]
    JOBS = len(jobs)
    ops, loads, per_slot = [], [], [0] * DEPTH
    for j, (w, t, c) in enumerate(jobs):
        ops.append((ops[-1] if ops else 0) + (2 if w == "col" and kind == "snake" else 1))
        per_slot[j % DEPTH] += 1 if w == "col" and K > 1 else 0
        per_slot[j % DEPTH] += 1 if w == "col" else (3 if K > 1 else 2)
        loads.append(per_slot[j % DEPTH])
    OPS = ops[-1]
    assert JOBS % DEPTH == 0
    jobs_at = [range(JOBS * c // NB, JOBS * (c + 1) // NB) for c in range(NB)]
    MATES = {0: (0, 1), 1: (0, 1, 2), 2: (1, 2)}
    with ExitStack() as ctx:
        sem = stage_semaphores(nc, ctx, names)
        job_in = [sem["job_in0"], sem["job_in1"], sem["job_in2"]]
        gate_in = [sem["gate_in0"], sem["gate_in1"]]

        def sb(name, shape, dt=F32):
            return ctx.enter_context(nc.sbuf_tensor(name + W["tag"], shape, dt))
        ya = [sb(f"ya{j}", [P, CH]) for j in range(DEPTH)]
        yb = [sb(f"yb{j}", [P, CH]) for j in range(DEPTH)]
        ub = [sb(f"ub{j}", [P, CH]) for j in range(DEPTH)]
        total = [sb(f"total{j}", [P, TILES, L]) for j in range(2)]
        xr = sb("xr", [DM, 2, L])
        wo = sb("wo", [P, TILES * DM])
        ds = sb("ds", [P, TILES * K])
        dsum = sb("dsum", [P, TILES])
        lng, lnb = (sb(n, [P, TILES]) for n in ("lng", "lnb"))
        centre_by = sb("centre_by", [P, TILES, TILES, P])
        average_by = sb("average_by", [P, TILES, 2])
        spread_by = sb("spread_by", [2, TILES, P])
        zc = [sb(f"zc{j}", [P, TILES, BANK]) for j in range(2)]
        sq = sb("sq", [P, TILES, BANK])
        root = sb("root", [2, BANK])
        tn = [sb(f"tn{j}", [P, TILES, BANK]) for j in range(2)]
        ob = sb("ob", [P, 2, 4, DM])
        cent = ctx.enter_context(nc.psum_tensor("cent" + W["tag"], [P, TILES, BANK], F32))
        scale = ctx.enter_context(nc.psum_tensor("scale" + W["tag"], [P, TILES, BANK], F32))
        outp = ctx.enter_context(nc.psum_tensor("outp" + W["tag"], [P, 2, BANK], F32))
        y_v = yseq.rearrange("(k p c) t q l -> k p c t q l", p=PAIRS, c=NCH)
        u_v = useq.rearrange("(k p c) t q l -> k p c t q l", p=PAIRS, c=NCH)


        def residual(dve, p, c):
            if last:
                return
            dve.wait_ge(sem["out_full"], p * NB + (c + 3))
            if c == 0:
                dve.wait_ge(sem["x_in"], p * 16 + 16)
            for b in range(2):
                img = xr[:, b, :].rearrange("q (h w) -> q h w", w=SIDE)
                src = outp[0:DM, b, :].rearrange("q (h w) -> q h w", w=SIDE)
                a = c * ROWS_PER_BANK
                for cols, view in first_order(kind, img, (a, a + ROWS_PER_BANK)):
                    ins = dve.tensor_tensor(view, view, src[:, :, cols], ALU.add)
            ins.then_inc(sem["x_done"], 1)

        with nc.Block() as block:
            @block.sync
            def _(sp):
                def load_job(pair, count, j):
                    w, t, c = jobs[j]
                    s = j % DEPTH
                    if j >= DEPTH:
                        sp.wait_ge(sem["total_step"], count * OPS + ops[j - DEPTH])
                    elif not isinstance(count, int):
                        sp.wait_ge(sem["total_step"], count * OPS + (ops[j - DEPTH] - OPS))
                    first = 0 if w == "row" else 1
                    sp.dma_start(ya[s][:], y_v[first, pair, c, t]).then_inc(job_in[s], 16)
                    if K > 1:
                        sp.dma_start(yb[s][:], y_v[first + 2, pair, c, t]).then_inc(job_in[s], 16)
                    if w == "row":
                        sp.dma_start(ub[s][:], u_v[0, pair, c, t]).then_inc(job_in[s], 16)

                def load_gate(p, c):
                    sp.wait_ge(sem["gated"], p * NB + (c + 1))
                    sp.dma_start(zc[c % 2][:], zgate[p, c].rearrange("t q l -> q t l")).then_inc(gate_in[c % 2], 16)

                def store_tokens(p, c):
                    sp.wait_ge(sem["x_done"], p * NB + (c + 2))
                    for b in range(2):
                        sp.dma_start(out[p * 2 + b, c * BANK:(c + 1) * BANK, :].rearrange("(j q) d -> q j d", q=P),
                                     ob[:, b]).then_inc(sem["out_stored"], 16)

                for dst, name in ((wo, "wo"), (ds, "ds"), (lng, "lng"), (lnb, "lnb"), (centre_by, "centre"),
                                  (average_by, "average"), (spread_by, "spread")):
                    sp.dma_start(dst[:], W[name]).then_inc(sem["w_in"], 16)
                for j in range(JOBS):
                    load_job(0, 0, j)
                with sp.Fori(0, PAIRS // 2) as i:
                    for half in range(2):
                        p = i * 2 + half
                        load_gate(p, 0)
                        for c in range(NB):
                            for j in jobs_at[c]:
                                load_job((p + 1) % PAIRS, p + 1, j)
                            if c == 0:
                                sp.wait_ge(sem["x_free"], p + 1)
                                sp.dma_start(xr[:], x_t[bass.ds(2 * p, 2)].rearrange("b c l -> c b l"))\
                                    .then_inc(sem["x_in"], 16)
                            if c + 1 < NB:
                                load_gate(p, c + 1)
                            if last and c > 0:
                                store_tokens(p, c - 1)
                        if last:
                            store_tokens(p, NB - 1)
                        else:
                            sp.wait_ge(sem["x_done"], p * NB + (NB + 1))
                            sp.dma_start(x_t[bass.ds(2 * p, 2)].rearrange("b c l -> c b l"), xr[:])\
                                .then_inc(sem["x_stored"], 16)
                            sp.wait_ge(sem["x_stored"], p * 16 + 16)
                            sp.sem_inc(sem["x_free"], 1)
                if last:
                    sp.wait_ge(sem["out_stored"], 32 * PAIRS * NB + 32)
                else:
                    sp.wait_ge(sem["x_stored"], 16 * PAIRS)

            @block.tensor
            def _(pe):
                def centre(p, c, half):
                    if c == 0:
                        pe.wait_ge(sem["total_step"], p * OPS + OPS)
                    pe.wait_ge(sem["copied"], p * NB + (c + 1))
                    for d in range(TILES):
                        for n, s in enumerate(MATES[d]):
                            mm = pe.matmul(cent[:, d, :], centre_by[:, s, d, :],
                                           total[half][:, s, c * BANK:(c + 1) * BANK],
                                           start=(n == 0), stop=(n == len(MATES[d]) - 1))
                    mm.then_inc(sem["centred_full"], 1)

                def variance(p, c):
                    pe.wait_ge(sem["squared"], p * NB + (c + 1))
                    pe.wait_ge(sem["normed"], p * NB + (c + 1))
                    for s in range(TILES):
                        mm = pe.matmul(scale[0:2, 0, :], average_by[:, s, :], sq[:, s, :], start=(s == 0),
                                       stop=(s == TILES - 1))
                    mm.then_inc(sem["var_full"], 1)

                def spread(p, c):
                    pe.wait_ge(sem["inverted"], p * NB + (c + 1))
                    for s in range(TILES):
                        mm = pe.matmul(scale[:, s, :], spread_by[:, s, :], root[:, :], start=True, stop=True)
                    mm.then_inc(sem["spread"], 1)

                def project(p, c):
                    pe.wait_ge(sem["gated"], p * NB + (c + 3))
                    pe.wait_ge(sem["x_done"], p * NB + (c + 1))
                    if last and c == 0:
                        pe.wait_ge(sem["x_in"], p * 16 + 16)
                    g = tn[c % 2]
                    for b in range(2):
                        rows = slice(64 * b, 64 * b + 64)
                        if not last:
                            pe.matmul(outp[0:DM, b, :], wo[:, 2 * b * DM:(2 * b + 1) * DM], g[:, 2 * b, :],
                                      start=True, stop=False)
                            mm = pe.matmul(outp[0:DM, b, :], wo[rows, DM:2 * DM], g[rows, 1, :],
                                           start=False, stop=True)
                        else:
                            for j in range(4):
                                o = outp[:, b, j * DM:(j + 1) * DM]
                                tok = slice(j * P, (j + 1) * P)
                                pe.matmul(o, g[:, 2 * b, tok], wo[:, 2 * b * DM:(2 * b + 1) * DM],
                                          start=True, stop=False)
                                pe.matmul(o, g[rows, 1, tok], wo[rows, DM:2 * DM], start=False, stop=False)
                                mm = pe.matmul(o, xr[:, b, c * BANK + j * P:c * BANK + (j + 1) * P],
                                               T["ident"][0:DM, 0:DM], start=False, stop=True)
                    mm.then_inc(sem["out_full"], 1)

                pe.sem_inc(sem["out_full"], 2)
                pe.sem_inc(sem["var_full"], 1)
                pe.sem_inc(sem["spread"], 1)
                pe.wait_ge(sem["w_in"], 112)
                with pe.Fori(0, PAIRS // 2) as i:
                    for half in range(2):
                        p = i * 2 + half
                        if norm:
                            centre(p, 0, half)
                        for c in range(NB):
                            if norm:
                                variance(p, c)
                                if c + 1 < NB:
                                    centre(p, c + 1, half)
                                spread(p, c)
                                if c:
                                    project(p, c - 1)
                            else:
                                project(p, c)
                        if norm:
                            project(p, NB - 1)
                        if last:
                            pe.wait_ge(sem["out_full"], p * NB + (NB + 2))
                            pe.sem_inc(sem["x_free"], 1)

            @block.scalar
            def _(act):
                def square(p, c):
                    act.wait_ge(sem["centred_full"], p * NB + (c + 2))
                    act.wait_ge(sem["var_full"], p * NB + (c + 1))
                    act.activation(sq[:], cent[:], ACT.Square).then_inc(sem["squared"], 1)

                def take(p, c):
                    act.wait_ge(sem["out_full"], p * NB + (c + 1))
                    act.copy(tn[c % 2][:], cent[:]).then_inc(sem["copied"], 1)

                def deviation(p, c):
                    act.wait_ge(sem["spread"], p * NB + (c + 1))
                    act.wait_ge(sem["var_full"], p * NB + (c + 2))
                    act.activation(root[:], scale[0:2, 0, :], ACT.Sqrt, bias=T["eps"][0:2, 0:1])\
                        .then_inc(sem["rooted"], 1)

                def gain(p, c):
                    act.wait_ge(sem["normed"], p * NB + (c + 2))
                    for t in range(TILES):
                        act.activation(tn[c % 2][:, t, :], tn[c % 2][:, t, :], ACT.Identity, bias=lnb[:, t:t + 1],
                                       scale=lng[:, t:t + 1]).then_inc(sem["affine"], 1)

                act.sem_inc(sem["copied"], 1)
                act.wait_ge(sem["w_in"], 112)
                if not norm and not last:
                    return
                with act.Fori(0, PAIRS // 2) as i:
                    for half in range(2):
                        p = i * 2 + half
                        if norm:
                            square(p, 0)
                            take(p, 0)
                        for c in range(NB):
                            if norm:
                                deviation(p, c)
                                if c + 1 < NB:
                                    square(p, c + 1)
                                gain(p, c)
                                if c + 1 < NB:
                                    take(p, c + 1)
                            if last:
                                act.wait_ge(sem["out_full"], p * NB + (c + 3))
                                act.wait_ge(sem["out_stored"], p * (32 * NB) + 32 * (c + 1))
                                act.copy(ob[:].rearrange("q b j d -> q b (j d)"), outp[:, :, 0:4 * DM])\
                                    .then_inc(sem["x_done"], 1)

            @block.vector
            def _(dve):
                def add_job(count, j):
                    w, t, c = jobs[j]
                    s = j % DEPTH
                    if K > 1:
                        dve.wait_ge(sem["paired"], count * JOBS + (j + 1))
                    else:
                        dve.wait_ge(job_in[s], count * (16 * per_slot[s]) + 16 * loads[j])
                    acc = total[count_half(count)][:, t, :]
                    if w == "row":
                        if not isinstance(count, int) and j == 0:
                            if norm:
                                dve.wait_ge(sem["centred_full"], (count - 1) * NB + 1)
                            else:
                                dve.wait_ge(sem["gated"], (count - 1) * NB + 2)
                        dve.scalar_tensor_tensor(out=acc[:, c * CH:(c + 1) * CH], in0=ub[s][:],
                                                 scalar=dsum[:, t:t + 1], in1=ya[s][:], op0=ALU.mult,
                                                 op1=ALU.add).then_inc(sem["total_step"], 1)
                        return
                    wide = CH // SIDE
                    col = ya[s][:].rearrange("q (w h) -> q w h", h=SIDE)
                    img = acc.rearrange("q (h w) -> q h w", w=SIDE)
                    for n, (rows, view) in enumerate(column_order(kind, img)):
                        dve.wait_ge(sem["total_step"], count * OPS + (ops[j - 1] + n))
                        part = view[:, c * wide:(c + 1) * wide, :]
                        dve.tensor_tensor(part, part, col[:, :, rows], ALU.add).then_inc(sem["total_step"], 1)

                def count_half(count):
                    return 0 if isinstance(count, int) else (half + 1) % 2

                dve.sem_inc(sem["centred_full"], 1)
                dve.sem_inc(sem["normed"], 1)
                dve.sem_inc(sem["x_done"], 1)
                dve.sem_inc(sem["x_free"], 1)
                dve.sem_inc(sem["out_stored"], 32)
                dve.wait_ge(sem["w_in"], 112)
                dve.tensor_reduce(dsum[:], ds[:].rearrange("q (t k) -> q t k", k=K), mybir.AxisListType.X, ALU.add)\
                    .then_inc(sem["dsum"], 1)
                dve.wait_ge(sem["dsum"], 1)
                for j in range(JOBS):
                    add_job(0, j)
                with dve.Fori(0, PAIRS // 2) as i:
                    for half in range(2):
                        p = i * 2 + half
                        for c in range(NB):
                            now = list(jobs_at[c])
                            if norm:
                                dve.wait_ge(sem["rooted"], p * NB + (c + 1))
                                dve.reciprocal(root[:], root[:]).then_inc(sem["inverted"], 1)
                                if now:
                                    add_job(p + 1, now.pop(0))
                                dve.wait_ge(sem["copied"], p * NB + (c + 2))
                                dve.wait_ge(sem["spread"], p * NB + (c + 2))
                                dve.tensor_tensor(tn[c % 2][:], tn[c % 2][:], scale[:], ALU.mult)\
                                    .then_inc(sem["normed"], 1)
                            for j in now:
                                add_job(p + 1, j)
                            if c:
                                residual(dve, p, c - 1)
                        residual(dve, p, NB - 1)

            @block.gpsimd
            def _(pool):
                def pair_up(count, j):
                    if K == 1:
                        return
                    s = j % DEPTH
                    pool.wait_ge(job_in[s], count * (16 * per_slot[s]) + 16 * loads[j])
                    pool.tensor_tensor(ya[s][:], ya[s][:], yb[s][:], ALU.add).then_inc(sem["paired"], 1)

                pool.sem_inc(sem["gated"], 2)
                for j in range(JOBS):
                    pair_up(0, j)
                with pool.Fori(0, PAIRS // 2) as i:
                    for half in range(2):
                        p = i * 2 + half
                        for c in range(NB):
                            for j in jobs_at[c]:
                                pair_up(p + 1, j)
                            if norm:
                                pool.wait_ge(sem["affine"], p * (TILES * NB) + TILES * (c + 1))
                                src = tn[c % 2][:]
                            else:
                                if c == 0:
                                    pool.wait_ge(sem["total_step"], p * OPS + OPS)
                                pool.wait_ge(sem["out_full"], p * NB + (c + 1))
                                src = total[half][:, :, c * BANK:(c + 1) * BANK]
                            pool.wait_ge(gate_in[c % 2], p * (8 * NB) + 16 * (c // 2 + 1))
                            pool.tensor_tensor(tn[c % 2][:], src, zc[c % 2][:], ALU.mult).then_inc(sem["gated"], 1)
        clear(nc, sem)


def build(nc, args, out, layers=(0, 1, 2, 3)):
    names = ("win", "convw", "convb", "wx", "wdt", "bdt", "a_log", "ds", "lng", "lnb", "wo")
    shared = {k: args[k] for k in ("pick", "centre", "average", "spread")}
    W = {n: {"tag": f"_{n}", **shared, **{k: args[f"{k}{n}"] for k in names}} for n in layers}
    x_t = nc.dram_tensor("x_t", [NBATCH, DM, L], F32, kind="Internal").ap()
    chunks = 4 * PAIRS * NCH
    useq = nc.dram_tensor("useq", [chunks // 2, TILES, P, CH], F32, kind="Internal").ap()
    yseq = nc.dram_tensor("yseq", [chunks, TILES, P, CH], F32, kind="Internal").ap()
    zgate = nc.dram_tensor("zgate", [PAIRS, BANKS_L, TILES, P, BANK], F32, kind="Internal").ap()
    neg_a = {n: nc.dram_tensor(f"neg_a{n}", [DIRS[KINDS[n]], P, TILES * NS], F32, kind="Internal").ap()
             for n in layers}
    with ExitStack() as ctx:
        T = {}
        for name, shape, dt in (("ident", [P, P], F32), ("group", [DM, DM], F32),
                                ("eps", [P, 1], F32), ("zeros", [P, 2 * TILES * NS], F32)):
            T[name] = ctx.enter_context(nc.sbuf_tensor(f"t_{name}", shape, dt))
        loaded = ctx.enter_context(nc.semaphore("tables_in"))
        filled = ctx.enter_context(nc.semaphore("tables_filled"))
        with nc.Block() as block:
            @block.sync
            def _(sp):
                for name in ("ident", "group"):
                    sp.dma_start(T[name][:], args[name]).then_inc(loaded, 16)
                sp.wait_ge(loaded, 32)

            @block.vector
            def _(dve):
                dve.memset(T["eps"][:], LN_EPS).then_inc(filled, 1)
                dve.memset(T["zeros"][:], 0.0).then_inc(filled, 1)
                dve.wait_ge(filled, 2)
        setup_stage(nc, T, W, layers, neg_a)
        to_channels_stage(nc, T, args["x"], x_t)
        for n in layers:
            kind = KINDS[n]
            count = SEQS[kind] * PAIRS * NCH
            results = DIRS[kind] * PAIRS * NCH
            expand_stage(nc, kind, T, W[n], x_t, useq[0:count], zgate)
            scan_stage(nc, kind, T, W[n], useq[0:count], neg_a[n], yseq[0:results])
            merge_stage(nc, kind, T, W[n], useq[0:count], yseq[0:results], zgate, x_t, out, n == layers[-1])


def tiles(a):
    return np.stack([a[:P], np.concatenate([a[P:], a[P:]]), a[:P]], axis=1)


def constants():
    batch = np.stack([np.zeros(P), np.repeat([0, 1], 64), np.ones(P)], axis=1)
    same = (batch[:, :, None, None] == batch.T[None, None]).astype(np.float32)
    eye = np.zeros((P, TILES, TILES, P), np.float32)
    for t in range(TILES):
        eye[:, t, t] = np.eye(P)
    one = 0x3F80
    pick = np.zeros((3, 2, NS, TILES, NS, P), np.uint16)
    for b in range(2):
        for n in range(NS):
            pick[:, b, n, :, n] = one * (batch.T == b)
    group = np.kron(np.eye(DM // 3), np.ones((3, 3))) / 3
    return {
        "ident": np.eye(P, dtype=np.float32),
        "pick": pick.reshape(96, TILES, NS, P),
        "group": group.astype(np.float32),
        "average": (np.stack([batch == 0, batch == 1], axis=-1) / DI).astype(np.float32),
        "spread": np.stack([batch.T == 0, batch.T == 1]).astype(np.float32),
        "centre": (eye - same / DI).astype(np.float32),
    }


def layer_arrays(n, w):
    K = DIRS[KINDS[n]]
    xp, dt, db, al, dsk = w["xp"], w["dt"], w["db"], w["al"], w["ds"]
    R = dt.shape[2]
    wx = np.zeros((K, P, TILES, 96), np.float32)
    wdt = np.zeros((K, 32, TILES, P), np.float32)
    for b in range(2):
        rows = slice(64 * b, 64 * b + 64)
        for k in range(K):
            for cols, src in ((slice(NS * b, NS * b + NS), xp[k, R:R + NS]),
                              (slice(32 + NS * b, 32 + NS * b + NS), xp[k, R + NS:]),
                              (slice(64 + RMAX * b, 64 + RMAX * b + R), xp[k, :R])):
                wx[k, :, 2 * b, cols] = src[:, :P].T
                wx[k, rows, 1, cols] = src[:, P:].T
            r = slice(RMAX * b, RMAX * b + R)
            wdt[k, r, 2 * b, :] = dt[k, :P].T
            wdt[k, r, 1, rows] = dt[k, P:].T
    per_dir = lambda a: np.stack([tiles(a[k]) for k in range(K)])
    arrays = {
        "win": w["win"].T,
        "convw": tiles(w["cw"].reshape(DI, -1)).reshape(P, -1),
        "convb": tiles(w["cb"]),
        "wx": wx, "wdt": wdt, "bdt": per_dir(db),
        "a_log": per_dir(al.reshape(K, DI, NS)).transpose(1, 0, 2, 3).reshape(P, -1),
        "ds": tiles(dsk.reshape(K, DI).T).reshape(P, -1),
        "lng": tiles(w["lng"]), "lnb": tiles(w["lnb"]),
        "wo": tiles(w["wo"].T).reshape(P, -1),
    }
    return {f"{k}{n}": np.ascontiguousarray(v) for k, v in arrays.items()}


def layout(v, layers=(0, 1, 2, 3)):
    arrays = {"x": np.ascontiguousarray(v["x"]).reshape(NBATCH, L, DM), **constants()}
    keys = [
        dict(win="in_proj_w", cw="conv_w", cb="conv_b", xp="x_proj_w", dt="dt_proj_w", db="dt_proj_b", al="A_logs",
             ds="Ds", lng="ln_gamma", lnb="ln_beta", wo="out_proj_w"),
        dict(win="in_proj_w", cw="conv_w", cb="conv_b", xp="x_proj_weight", dt="dt_projs_weight",
             db="dt_projs_bias", al="A_logs", ds="Ds", lng="out_norm_w", lnb="out_norm_b", wo="out_proj_w"),
        dict(win="in_proj_w", cw="conv_w", cb="conv_b", xp="x_proj_w", dt="dt_projs_w", db="dt_projs_b",
             al="A_logs", ds="Ds", lng="ln_g", lnb="ln_b", wo="out_proj_w"),
        dict(win="W_in", cw="conv_w", cb="conv_b", xp="W_x", dt="W_dt", db="b_dt", al="A_log", ds="D",
             lng="D", lnb="D", wo="W_out"),
    ]
    for n in layers:
        w = {k: np.asarray(v[f"L{n}_conv_{name}"]) for k, name in keys[n].items()}
        if n == 3:
            w.update({k: w[k][None] for k in ("xp", "dt", "db")})
        arrays.update(layer_arrays(n, w))
    return arrays


def kernel(**inputs):
    import concourse.bacc as bacc
    from concourse.bass_utils import run_bass_kernel_spmd

    nc = bacc.Bacc("TRN2", target_bir_lowering=False, num_devices=1)
    arrays = layout(inputs)
    args = {k: nc.dram_tensor(f"in_{k}", a.shape, mybir.dt.from_np(a.dtype), kind="ExternalInput").ap()
            for k, a in arrays.items()}
    out = nc.dram_tensor("out", [NBATCH, L, DM], F32, kind="ExternalOutput").ap()
    build(nc, args, out)
    r = run_bass_kernel_spmd(nc, [{f"in_{k}": a for k, a in arrays.items()}], core_ids=[0])
    return r.results[0]["out"].reshape(NBATCH, SIDE, SIDE, DM)
```
